# Optimizing a Trainium2 kernel written in Bass

```python
import numpy as np
import jax
import jax.numpy as jnp

def _softmax(x, axis=-1):
    return jax.nn.softmax(x, axis=axis)

def _gelu(x):
    return jax.nn.gelu(x, approximate=True)

def _silu(x):
    return jax.nn.silu(x)

def _sigmoid(x):
    return jax.nn.sigmoid(x)

def _layernorm(x, axis=-1, eps=1e-05):
    m = jnp.mean(x, axis=axis, keepdims=True)
    v = jnp.var(x, axis=axis, keepdims=True)
    return (x - m) / jnp.sqrt(v + eps)

def _scatter_add(tgt, idx, src, axis=0):
    return tgt.at[idx].add(src)

def _segment_sum(src, seg, n):
    return jax.ops.segment_sum(src, seg, n)
kernel_name = 'mk_gnn_preln_d4_gnn_r8_204017'

def setup_inputs(seed: int=0):
    np.random.seed(seed)
    _w = jnp.asarray

    def _rec_inputs():
        import jax
        import jax.numpy as jnp
        _gk = jax.random.key(seed)
        x = 0.0004528 + 0.9998 * jax.random.normal(jax.random.fold_in(_gk, 1), (12500, 32), jnp.float32)
        _s = jax.random.randint(jax.random.fold_in(_gk, 2), (200000,), 0, 12500, jnp.int32)
        _d = jax.random.randint(jax.random.fold_in(_gk, 3), (200000,), 0, 12500, jnp.int32)
        _loop = jnp.arange(12500, dtype=jnp.int32)
        src = jnp.concatenate([_s, _d, _loop])
        dst = jnp.concatenate([_d, _s, _loop])
        _o = jnp.argsort(dst, stable=True)
        src = src[_o]
        dst = dst[_o]
        edge_attr_32 = 0.000216709 + 1.00012 * jax.random.normal(jax.random.fold_in(_gk, 12), (412500, 32), jnp.float32)
        edge_attr_4 = 0.000714719 + 1.00021 * jax.random.normal(jax.random.fold_in(_gk, 13), (412500, 4), jnp.float32)
        return (x, src, dst, edge_attr_32, edge_attr_4)
    x, src, dst, edge_attr_32, edge_attr_4 = _rec_inputs()

    def _L0_gnn_setup():
        import jax, jax.numpy as jnp
        import numpy as np
        N_GRAPHS = 10
        N_PER = 625
        DEG = 32
        IN_DIM = 32
        HID_DIM = 128
        OUT_DIM = 32

        def _gcn_left(h, W, b, src, dst, deg_inv, N):
            h = h * deg_inv[:, None]
            h = h @ W
            agg = jax.ops.segment_sum(h[src], dst, num_segments=N)
            return agg + b
        key = jax.random.key(seed)
        k0, k1, k2, k3, k4 = jax.random.split(key, 5)
        N = N_GRAPHS * N_PER
        E = N * DEG
        src_local = jax.random.randint(k0, (E,), 0, N_PER)
        dst_local = jax.random.randint(k1, (E,), 0, N_PER)
        offs = jnp.repeat(jnp.arange(N_GRAPHS) * N_PER, N_PER * DEG)
        src = (src_local + offs).astype(jnp.int64) if jax.config.jax_enable_x64 else src_local + offs
        dst = (dst_local + offs).astype(src.dtype)
        x = jax.random.normal(k2, (N, IN_DIM), dtype=jnp.float32)
        W1 = jax.random.normal(k3, (IN_DIM, HID_DIM), dtype=jnp.float32) / np.sqrt(IN_DIM)
        b1 = jnp.zeros((HID_DIM,), dtype=jnp.float32)
        W2 = jax.random.normal(k4, (HID_DIM, OUT_DIM), dtype=jnp.float32) / np.sqrt(HID_DIM)
        b2 = jnp.zeros((OUT_DIM,), dtype=jnp.float32)
        eye = jnp.eye(IN_DIM, dtype=jnp.float32)
        J = jnp.concatenate([eye[IN_DIM // 2:], -eye[:IN_DIM // 2]], axis=0)
        return {'x': x, 'W1': W1, 'b1': b1, 'W2': W2, 'b2': b2, 'J': J, 'src': src, 'dst': dst}
    _L0_gnn_all = _L0_gnn_setup()
    _L0_gnn_in = {k: v for k, v in _L0_gnn_all.items() if k in ('W1', 'b1', 'W2', 'b2', 'J')}
    del _L0_gnn_all

    def _L1_gnn_setup():
        import jax, jax.numpy as jnp
        import numpy as np
        MUL = 8
        N_NODES = 12500
        N_EDGES = 100000
        EDGE_DIM = 32
        MLP_DIM = 64
        W_NUMEL = 4 * MUL * MUL
        ALPHA = 0.25
        C110 = 1.0 / np.sqrt(3.0)
        SI_SCALE = 1.0 / np.sqrt(MUL)
        key = jax.random.key(seed)
        ks = jax.random.split(key, 10)
        node_attr = jax.random.normal(ks[0], (N_NODES, 4 * MUL), dtype=jnp.float32)
        edge_index = jax.random.randint(ks[1], (2, N_EDGES), 0, N_NODES, dtype=jnp.int64)
        edge_sh = jax.random.normal(ks[2], (N_EDGES, 4), dtype=jnp.float32)
        edge_feat = jax.random.normal(ks[3], (N_EDGES, EDGE_DIM), dtype=jnp.float32)
        W1 = jax.random.normal(ks[4], (EDGE_DIM, MLP_DIM), dtype=jnp.float32) / np.sqrt(EDGE_DIM)
        b1 = jnp.zeros((MLP_DIM,), dtype=jnp.float32)
        W2 = jax.random.normal(ks[5], (MLP_DIM, W_NUMEL), dtype=jnp.float32) / np.sqrt(MLP_DIM)
        b2 = jnp.zeros((W_NUMEL,), dtype=jnp.float32)
        si_w0 = jax.random.normal(ks[6], (MUL, MUL), dtype=jnp.float32)
        si_w1 = jax.random.normal(ks[7], (MUL, MUL), dtype=jnp.float32)
        return {'node_attr': node_attr, 'edge_index': edge_index, 'edge_sh': edge_sh, 'edge_feat': edge_feat, 'W1': W1, 'b1': b1, 'W2': W2, 'b2': b2, 'si_w0': si_w0, 'si_w1': si_w1}
    _L1_gnn_all = _L1_gnn_setup()
    _L1_gnn_in = {k: v for k, v in _L1_gnn_all.items() if k in ('W1', 'b1', 'W2', 'b2', 'si_w0', 'si_w1')}
    del _L1_gnn_all

    def _L2_gnn_setup():
        import jax, jax.numpy as jnp
        import numpy as np
        N = 12500
        E = 200000
        F_IN = 32
        F_OUT = 32
        key = jax.random.key(seed)
        k1, k2, k3, k4, k5 = jax.random.split(key, 5)
        x = jax.random.normal(k1, (N, F_IN), dtype=jnp.float32)
        edge_src = jax.random.randint(k2, (E,), 0, N, dtype=jnp.int32)
        edge_dst = jax.random.randint(k3, (E,), 0, N, dtype=jnp.int32)
        bound = 1.0 / np.sqrt(2 * F_IN)
        W = jax.random.uniform(k4, (2 * F_IN, F_OUT), minval=-bound, maxval=bound, dtype=jnp.float32)
        b = jax.random.uniform(k5, (F_OUT,), minval=-bound, maxval=bound, dtype=jnp.float32)
        return {'x': x, 'W': W, 'b': b, 'edge_src': edge_src, 'edge_dst': edge_dst}
    _L2_gnn_all = _L2_gnn_setup()
    _L2_gnn_in = {k: v for k, v in _L2_gnn_all.items() if k in ('W', 'b')}
    del _L2_gnn_all

    def _L3_gnn_setup():
        import jax, jax.numpy as jnp
        import numpy as np
        N = 12500
        E = 200000
        D = 32
        key = jax.random.key(seed)
        k_x, k_e, kq, kk, kv, ko = jax.random.split(key, 6)
        s = 1.0 / np.sqrt(D).astype(np.float32)
        x = jax.random.normal(k_x, (N, D), dtype=jnp.float32)
        edge_index = jax.random.randint(k_e, (2, E), 0, N, dtype=jnp.int64)
        Wq = jax.random.normal(kq, (D, D), dtype=jnp.float32) * s
        Wk = jax.random.normal(kk, (D, D), dtype=jnp.float32) * s
        Wv = jax.random.normal(kv, (D, D), dtype=jnp.float32) * s
        Wo = jax.random.normal(ko, (D, D), dtype=jnp.float32) * s
        return {'x': x, 'edge_index': edge_index, 'Wq': Wq, 'Wk': Wk, 'Wv': Wv, 'Wo': Wo}
    _L3_gnn_all = _L3_gnn_setup()
    _L3_gnn_in = {k: v for k, v in _L3_gnn_all.items() if k in ('Wq', 'Wk', 'Wv', 'Wo')}
    del _L3_gnn_all
    return {'x': x, 'src': src, 'dst': dst, 'edge_attr_32': edge_attr_32, 'edge_attr_4': edge_attr_4, 'L0_gnn_W1': _L0_gnn_in['W1'], 'L0_gnn_b1': _L0_gnn_in['b1'], 'L0_gnn_W2': _L0_gnn_in['W2'], 'L0_gnn_b2': _L0_gnn_in['b2'], 'L0_gnn_J': _L0_gnn_in['J'], 'L1_gnn_W1': _L1_gnn_in['W1'], 'L1_gnn_b1': _L1_gnn_in['b1'], 'L1_gnn_W2': _L1_gnn_in['W2'], 'L1_gnn_b2': _L1_gnn_in['b2'], 'L1_gnn_si_w0': _L1_gnn_in['si_w0'], 'L1_gnn_si_w1': _L1_gnn_in['si_w1'], 'L2_gnn_W': _L2_gnn_in['W'], 'L2_gnn_b': _L2_gnn_in['b'], 'L3_gnn_Wq': _L3_gnn_in['Wq'], 'L3_gnn_Wk': _L3_gnn_in['Wk'], 'L3_gnn_Wv': _L3_gnn_in['Wv'], 'L3_gnn_Wo': _L3_gnn_in['Wo']}

def reference(x, src, dst, edge_attr_32, edge_attr_4, L0_gnn_W1, L0_gnn_b1, L0_gnn_W2, L0_gnn_b2, L0_gnn_J, L1_gnn_W1, L1_gnn_b1, L1_gnn_W2, L1_gnn_b2, L1_gnn_si_w0, L1_gnn_si_w1, L2_gnn_W, L2_gnn_b, L3_gnn_Wq, L3_gnn_Wk, L3_gnn_Wv, L3_gnn_Wo):
    import jax
    import jax.numpy as jnp

    def _L0_gnn_ref(x, W1, b1, W2, b2, J, src, dst):
        import jax, jax.numpy as jnp
        import numpy as np
        N_GRAPHS = 10
        N_PER = 625
        DEG = 32
        IN_DIM = 32
        HID_DIM = 128
        OUT_DIM = 32

        def _gcn_left(h, W, b, src, dst, deg_inv, N):
            h = h * deg_inv[:, None]
            h = h @ W
            agg = jax.ops.segment_sum(h[src], dst, num_segments=N)
            return agg + b
        N = x.shape[0]
        E = src.shape[0]
        ones = jnp.ones((E,), dtype=x.dtype)
        deg_out = jax.ops.segment_sum(ones, src, num_segments=N)
        deg_inv = 1.0 / jnp.clip(deg_out, 1.0)

        def H_total(y):
            h = jnp.tanh(_gcn_left(y, W1, b1, src, dst, deg_inv, N))
            out = _gcn_left(h, W2, b2, src, dst, deg_inv, N)
            return jnp.sum(deg_out[:, None] * out)
        dH = jax.grad(H_total)(x)
        return dH @ J.T

    def _L1_gnn_ref(node_attr, edge_index, edge_sh, edge_feat, W1, b1, W2, b2, si_w0, si_w1):
        import jax, jax.numpy as jnp
        import numpy as np
        MUL = 8
        N_NODES = 12500
        N_EDGES = 100000
        EDGE_DIM = 32
        MLP_DIM = 64
        W_NUMEL = 4 * MUL * MUL
        ALPHA = 0.25
        C110 = 1.0 / np.sqrt(3.0)
        SI_SCALE = 1.0 / np.sqrt(MUL)
        n = node_attr.shape[0]
        e = edge_sh.shape[0]
        h = jax.nn.relu(edge_feat @ W1 + b1)
        w = (h @ W2 + b2).reshape(e, 4, MUL, MUL)
        w_000, w_011, w_101, w_110 = (w[:, 0], w[:, 1], w[:, 2], w[:, 3])
        s = node_attr[:, :MUL]
        v = node_attr[:, MUL:].reshape(n, MUL, 3)
        src, dst = (edge_index[0], edge_index[1])
        s_e = s[src]
        v_e = v[src]
        sh0 = edge_sh[:, 0]
        sh1 = edge_sh[:, 1:4]
        m0 = ALPHA * (jnp.einsum('ei,eio->eo', s_e * sh0[:, None], w_000) + C110 * jnp.einsum('eim,em,eio->eo', v_e, sh1, w_110))
        m1 = ALPHA * (jnp.einsum('ei,em,eio->eom', s_e, sh1, w_011) + jnp.einsum('eim,eio->eom', v_e * sh0[:, None, None], w_101))
        out0 = jax.ops.segment_sum(m0, dst, num_segments=n)
        out1 = jax.ops.segment_sum(m1.reshape(e, MUL * 3), dst, num_segments=n).reshape(n, MUL, 3)
        out0 = out0 + SI_SCALE * (s @ si_w0)
        out1 = out1 + SI_SCALE * jnp.einsum('nim,io->nom', v, si_w1)
        return jnp.concatenate([out0, out1.reshape(n, MUL * 3)], axis=-1)

    def _L2_gnn_ref(x, W, b, edge_src, edge_dst):
        import jax, jax.numpy as jnp
        import numpy as np
        N = 12500
        E = 200000
        F_IN = 32
        F_OUT = 32
        n = x.shape[0]
        msgs = x[edge_src]
        summed = jax.ops.segment_sum(msgs, edge_dst, num_segments=n)
        cnt = jax.ops.segment_sum(jnp.ones_like(edge_dst, dtype=x.dtype), edge_dst, num_segments=n)
        neigh_mean = summed / jnp.maximum(cnt, 1.0)[:, None]
        h = jnp.concatenate([x, neigh_mean], axis=1)
        return jax.nn.relu(h @ W + b)

    def _L3_gnn_ref(x, edge_index, Wq, Wk, Wv, Wo):
        import jax, jax.numpy as jnp
        import numpy as np
        N = 12500
        E = 200000
        D = 32
        sender, receiver = (edge_index[0], edge_index[1])
        n = x.shape[0]
        scale = x.shape[1] ** (-0.5)
        Q = x @ Wq
        K = x @ Wk
        V = x @ Wv
        scores = jnp.sum(Q[receiver] * K[sender], axis=1) * scale
        smax = jax.ops.segment_max(scores, receiver, num_segments=n)
        alpha = jnp.exp(scores - smax[receiver])
        Z = jax.ops.segment_sum(alpha, receiver, num_segments=n)
        alpha = alpha / (Z[receiver] + 1e-06)
        out = jax.ops.segment_sum(alpha[:, None] * V[sender], receiver, num_segments=n)
        return x + out @ Wo
    edge_index = jnp.stack([src, dst])
    h = jnp.maximum(_layernorm(x, axis=-1), 0.0)
    x = x + _L0_gnn_ref(h, L0_gnn_W1, L0_gnn_b1, L0_gnn_W2, L0_gnn_b2, L0_gnn_J, src, dst)
    h = jnp.maximum(_layernorm(x, axis=-1), 0.0)
    x = x + _L1_gnn_ref(h, edge_index, edge_attr_4, edge_attr_32, L1_gnn_W1, L1_gnn_b1, L1_gnn_W2, L1_gnn_b2, L1_gnn_si_w0, L1_gnn_si_w1)
    h = jnp.maximum(_layernorm(x, axis=-1), 0.0)
    x = x + _L2_gnn_ref(h, L2_gnn_W, L2_gnn_b, src, dst)
    h = jnp.maximum(_layernorm(x, axis=-1), 0.0)
    x = x + _L3_gnn_ref(h, edge_index, L3_gnn_Wq, L3_gnn_Wk, L3_gnn_Wv, L3_gnn_Wo)
    return x

_drawn_inputs = setup_inputs


def setup_inputs(seed=0):
    import zlib

    import numpy as np

    out = dict(_drawn_inputs(seed))
    spreads = {'L0_gnn_b1': (0.0, 0.1),
     'L0_gnn_b2': (0.0, 0.1),
     'L1_gnn_b1': (0.0, 0.656),
     'L1_gnn_b2': (0.0, 0.405)}
    factors = {'L1_gnn_si_w0': 3.655,
     'L1_gnn_si_w1': 3.106,
     'L2_gnn_W': 7.841,
     'L2_gnn_b': 33.801,
     'L3_gnn_Wq': 64.0,
     'L3_gnn_Wk': 64.0}
    for name, (base, spread) in spreads.items():
        noise = np.random.default_rng([zlib.crc32(name.encode()), seed]).standard_normal(out[name].shape)
        drawn = base * np.exp(spread * noise) if base else spread * noise
        out[name] = jnp.asarray(drawn.astype(out[name].dtype))
    for name, factor in factors.items():
        out[name] = (out[name] * factor).astype(out[name].dtype)
    return out
```

```python
from contextlib import ExitStack

import concourse.bass as bass
import concourse.mybir as mybir

F32 = mybir.dt.float32
BF16 = mybir.dt.bfloat16
I32 = mybir.dt.int32
ALU = mybir.AluOpType
ACT = mybir.ActivationFunctionType
AX = mybir.AxisListType.X

P = 128
D = 32
N = 12500
NB = 100
NP = P * NB
E = 412500
C = 52
T = 3224
CHUNKS = T // C
ROUNDS = CHUNKS // 2
EP = P * T
S1 = C + 1
HG = 13
HGROUNDS = T // (2 * HG)
CHAINS = 8
NG = NB // 4
ACCROWS = NP + P
ZW = ACCROWS * D // P
EPS = 1e-5
BIG = 1e30
MAGIC = 1.5 * 2 ** 23
MUL, HID1, WN = 8, 64, 256
ALPHA, C110, SI_SCALE = 0.25, 3.0 ** -0.5, 8.0 ** -0.5
assert T % C == 0 and CHUNKS % 2 == 0 and T % (2 * HG) == 0 and C % 4 == 0 and EP >= E and ZW >= T


class Steps:

    def __init__(self):
        self.base, self.k, self.i, self.per = 0, 0, None, 0

    def enter(self, i, per):
        self.base, self.k, self.i, self.per = self.base + self.k, 0, i, per

    def leave(self, rounds):
        assert self.k == self.per, (self.k, self.per)
        self.base, self.k, self.i = self.base + rounds * self.per, 0, None

    def next(self):
        self.k += 1
        return self.base + self.k if self.i is None else self.i * self.per + (self.base + self.k)


def linker(eng, sem, steps):
    def link(ins):
        ins.then_inc(sem, 1)
        eng.wait_ge(sem, steps.next())
    return link


class Phase:

    def __init__(self, nc, name):
        self.nc, self.name, self.ctx, self.sems = nc, name, ExitStack(), []

    def __enter__(self):
        self.ctx.__enter__()
        return self

    def __exit__(self, *a):
        self.ctx.__exit__(*a)
        self.nc.clear_and_free_semaphores(self.sems)
        self.nc.all_engine_barrier()

    def sb(self, name, shape, dt=F32):
        return self.ctx.enter_context(self.nc.sbuf_tensor(f"{self.name}_{name}", shape, dt))

    def ps(self, name, shape, dt=F32):
        return self.ctx.enter_context(self.nc.psum_tensor(f"{self.name}_{name}", shape, dt))

    def sem(self, name):
        self.sems.append(self.nc.alloc_semaphore(f"{self.name}_{name}"))
        return self.sems[-1]


def cols(ap, i, n):
    return ap[:, bass.ds(i, n)]


def load_edges(nc, m, a):
    with Phase(nc, "ld") as ph:
        ids = ph.sb("ids", [P, 3, T], I32)
        before = ph.sb("before", [P, T])
        landed, zeroed, ready, zt, wr = (ph.sem(n) for n in ("landed", "zeroed", "ready", "zt", "wr"))
        consts, dv = ph.sem("consts"), ph.sem("dv")
        block = ph.ctx.enter_context(nc.Block())

        @block.sync
        def _(sp):
            sp.dma_start(ids[:, 0, :], a["dst"][1:1 + EP].rearrange("(p t) -> p t", p=P)).then_inc(landed, 16)
            sp.dma_start(ids[:, 1, :], a["dst"][0:EP].rearrange("(p t) -> p t", p=P)).then_inc(landed, 16)
            sp.dma_start(ids[:, 2, :], a["src"].rearrange("(p t) -> p t", p=P)).then_inc(landed, 16)
            sp.dma_start(m["X"][:, :, :], a["x"].rearrange("(p j) f -> p j f", p=P)).then_inc(landed, 16)
            sp.wait_ge(landed, 64)

        @block.scalar
        def _(act):
            act.wait_ge(zt, 1)
            ex = m["EX"][0:EP, :].rearrange("(p t) f -> p (t f)", p=P)
            for k in range(D):
                act.dma_start(ex[:, k * T:(k + 1) * T], m["zero"][:, 0:T]).then_inc(zeroed, 16)
            act.dma_start(m["EXD"][0:EP, :].rearrange("(p t) f -> p (t f)", p=P), m["zero"][:, 0:T]).then_inc(zeroed, 16)
            act.dma_start(m["SC"][EP:EP + 1, :], m["zero"][0:1, 0:D]).then_inc(zeroed, 16)
            act.dma_start(m["SC34"][EP:EP + 1, :], m["zero"][0:1, 0:D + 2]).then_inc(zeroed, 16)
            act.wait_ge(zeroed, 16 * (D + 3))

        @block.gpsimd
        def _(pool):
            pool.iota(m["iota"][:, :], pattern=[[1, P]], base=0, channel_multiplier=0,
                      allow_small_or_imprecise_dtypes=True).then_inc(consts, 1)
            pool.iota(m["rowid"][:, :], pattern=[[0, 1]], base=0, channel_multiplier=1,
                      allow_small_or_imprecise_dtypes=True).then_inc(consts, 1)

        @block.vector
        def _(dve):
            n = Steps()
            link = linker(dve, dv, n)
            nc.vector.memset(m["zero"][:, :], 0.0).then_inc(zt, 1)
            dve.wait_ge(consts, 2)
            nc.vector.tensor_copy(m["iotab"][:, :], m["iota"][:, :]).then_inc(ready, 1)
            nc.vector.tensor_scalar(m["ident"][:, :], m["iota"][:, :], m["rowid"][:, 0:1], None, ALU.is_equal).then_inc(ready, 1)
            nc.vector.tensor_scalar(m["below"][:, :], m["iota"][:, :], m["rowid"][:, 0:1], None, ALU.is_lt).then_inc(ready, 1)
            nc.vector.tensor_scalar(m["above"][:, :], m["iota"][:, :], m["rowid"][:, 0:1], None, ALU.is_gt).then_inc(ready, 1)
            dve.wait_ge(landed, 64)
            nc.vector.tensor_copy(m["dst0"][:, :], ids[:, 0, 0:1])
            nc.vector.tensor_copy(m["dstf"][:, :], ids[:, 0, :]).then_inc(ready, 1)
            link(nc.vector.tensor_copy(before[:, :], ids[:, 1, :]))
            nc.vector.tensor_copy(m["srcf"][:, :], ids[:, 2, :]).then_inc(ready, 1)
            dve.wait_ge(ready, 6)
            link(nc.vector.tensor_tensor(m["same"][:, :], m["dstf"][:, :], before[:, :], ALU.is_equal))
            link(nc.vector.tensor_reduce(m["whole"][:, :], m["same"][:, :], AX, ALU.min))


def histograms(nc, m):
    with Phase(nc, "hi") as ph:
        keyp = ph.sb("keyp", [P, 2, T], BF16)
        keyj = ph.sb("keyj", [P, 2, T], BF16)
        kf = ph.sb("kf", [P, T])
        kg = ph.sb("kg", [P, T])
        hotp = ph.sb("hotp", [P, 2, 2, HG, P], BF16)
        hotj = ph.sb("hotj", [P, 2, 2, HG, NB], BF16)
        zb = ph.sb("zb", [P, P], BF16)
        acc = [ph.ps(f"acc{k}", [P, 512]) for k in range(2)]
        dv, hot, used, zs, done, counted = (ph.sem(n) for n in ("dv", "hot", "used", "zs", "done", "counted"))
        block = ph.ctx.enter_context(nc.Block())

        @block.vector
        def _(dve):
            n = Steps()
            link = linker(dve, dv, n)
            nc.vector.memset(zb[:, :], 0.0).then_inc(zs, 1)
            for k, key in enumerate((m["dstf"], m["srcf"])):
                link(nc.vector.tensor_scalar(kf[:, :], key[:, :], 1.0 / NB, 0.5 / NB - 0.5, ALU.mult, ALU.add))
                link(nc.vector.tensor_scalar(kg[:, :], kf[:, :], MAGIC, -MAGIC, ALU.add, ALU.add))
                link(nc.vector.tensor_copy(keyp[:, k, :], kg[:, :]))
                link(nc.vector.scalar_tensor_tensor(kf[:, :], kg[:, :], -float(NB), key[:, :], ALU.mult, ALU.add))
                link(nc.vector.tensor_copy(keyj[:, k, :], kf[:, :]))
            with dve.Fori(0, HGROUNDS) as i:
                for b in range(2):
                    dve.wait_ge(used, i * 2 + b + 1)
                    for k in range(2):
                        nc.vector.tensor_tensor(
                            hotp[:, b, k, :, :], m["iotab"][:, None, :].to_broadcast([P, HG, P]),
                            keyp[:, k, bass.ds((i * 2 + b) * HG, HG)][:, :, None].to_broadcast([P, HG, P]),
                            ALU.is_equal).then_inc(hot, 1)
                        nc.vector.tensor_tensor(
                            hotj[:, b, k, :, :], m["iotab"][:, None, 0:NB].to_broadcast([P, HG, NB]),
                            keyj[:, k, bass.ds((i * 2 + b) * HG, HG)][:, :, None].to_broadcast([P, HG, NB]),
                            ALU.is_equal).then_inc(hot, 1)
            dve.wait_ge(done, 1)
            nc.vector.tensor_copy(m["cnt"][:, :], acc[0][:, 0:NB]).then_inc(counted, 1)
            nc.vector.tensor_copy(m["deg"][:, :], acc[1][:, 0:NB]).then_inc(counted, 1)

        @block.tensor
        def _(pe):
            pe.wait_ge(zs, 1)
            for k in range(2):
                nc.tensor.matmul(acc[k][:, 0:NB], zb[:, :], zb[:, 0:NB], start=True, stop=False).then_inc(used, 1)
            with pe.Fori(0, HGROUNDS) as i:
                for b in range(2):
                    pe.wait_ge(hot, (i * 2 + b + 1) * 4)
                    for k in range(2):
                        for c in range(HG):
                            last = nc.tensor.matmul(acc[k][:, 0:NB], hotp[:, b, k, c, :], hotj[:, b, k, c, :],
                                                    start=False, stop=False)
                    last.then_inc(used, 1)
            for k in range(2):
                last = nc.tensor.matmul(acc[k][:, 0:NB], zb[:, :], zb[:, 0:NB], start=False, stop=True)
            last.then_inc(done, 1)


def node_indices(nc, m, a):
    with Phase(nc, "ni") as ph:
        w = {k: ph.sb(k, [P, NB]) for k in ("scan", "end", "has", "pe", "t1", "t2", "t3")}
        zer = ph.sb("zer", [P, NB])
        tot = ph.sb("tot", [P, 1])
        off = ph.sb("off", [P, 1])
        tr = ph.sb("tr", [P, 1])
        offp = ph.ps("offp", [P, 512])
        dv, totals, offs, stored = (ph.sem(n) for n in ("dv", "totals", "offs", "stored"))
        block = ph.ctx.enter_context(nc.Block())

        @block.vector
        def _(dve):
            v = nc.vector
            n = Steps()
            link = linker(dve, dv, n)
            link(v.tensor_scalar(m["dinv"][:, :], m["deg"][:, :], 1.0, None, ALU.max))
            link(v.reciprocal(m["dinv"][:, :], m["dinv"][:, :]))
            link(v.tensor_scalar(m["cinv"][:, :], m["cnt"][:, :], 1.0, None, ALU.max))
            link(v.reciprocal(m["cinv"][:, :], m["cinv"][:, :]))
            link(v.memset(zer[:, :], 0.0))
            link(v.tensor_tensor_scan(w["scan"][:, :], m["cnt"][:, :], zer[:, :], 0.0, ALU.add, ALU.add))
            v.tensor_copy(tot[:, :], w["scan"][:, NB - 1:NB]).then_inc(totals, 1)
            dve.wait_ge(offs, 1)
            link(v.tensor_copy(off[:, :], offp[:, 0:1]))
            link(v.tensor_scalar(w["end"][:, :], w["scan"][:, :], off[:, 0:1], -1.0, ALU.add, ALU.add))
            link(v.tensor_tensor(w["t1"][:, :], w["end"][:, :], m["cnt"][:, :], ALU.subtract))
            link(v.tensor_scalar(w["t1"][:, :], w["t1"][:, :], 1.0, None, ALU.add))
            link(v.tensor_scalar(w["has"][:, :], m["cnt"][:, :], 0.5, None, ALU.is_gt))
            link(v.tensor_scalar(tr[:, :], m["rowid"][:, :], float(EP), None, ALU.add))
            link(v.tensor_scalar(w["t2"][:, :], w["t1"][:, :], tr[:, 0:1], None, ALU.subtract))
            link(v.tensor_tensor(w["t2"][:, :], w["t2"][:, :], w["has"][:, :], ALU.mult))
            link(v.tensor_scalar(w["t2"][:, :], w["t2"][:, :], tr[:, 0:1], None, ALU.add))
            link(v.tensor_copy(m["ixStart"][:, :], w["t2"][:, :]))
            link(v.tensor_scalar(w["t2"][:, :], w["end"][:, :], -float(EP), None, ALU.add))
            link(v.tensor_tensor(w["t2"][:, :], w["t2"][:, :], w["has"][:, :], ALU.mult))
            link(v.tensor_scalar(w["t2"][:, :], w["t2"][:, :], float(EP), None, ALU.add))
            link(v.tensor_copy(m["ixEnd"][:, :], w["t2"][:, :]))
            link(v.tensor_scalar(w["pe"][:, :], w["end"][:, :], 1.0 / T, 0.5 / T - 0.5, ALU.mult, ALU.add))
            link(v.tensor_scalar(w["pe"][:, :], w["pe"][:, :], MAGIC, -MAGIC, ALU.add, ALU.add))
            link(v.scalar_tensor_tensor(w["t3"][:, :], w["pe"][:, :], float(T), w["t1"][:, :], ALU.mult, ALU.is_gt))
            link(v.tensor_tensor(w["t3"][:, :], w["t3"][:, :], w["has"][:, :], ALU.mult))
            link(v.tensor_scalar(w["pe"][:, :], w["pe"][:, :], -float(P), None, ALU.add))
            link(v.tensor_tensor(w["pe"][:, :], w["pe"][:, :], w["t3"][:, :], ALU.mult))
            link(v.tensor_scalar(w["pe"][:, :], w["pe"][:, :], float(P), None, ALU.add))
            link(v.tensor_copy(m["ixCarry"][:, :], w["pe"][:, :]))

        @block.tensor
        def _(pe):
            pe.wait_ge(totals, 1)
            nc.tensor.matmul(offp[:, 0:1], m["above"][:, :], tot[:, :], start=True, stop=True).then_inc(offs, 1)

        @block.sync
        def _(sp):
            sp.dma_start(m["DEG"].rearrange("(p j) f -> p (j f)", p=P), m["deg"][:, :]).then_inc(stored, 16)
            sp.wait_ge(stored, 16)


def norm_relu(nc, m, name, x, out, table, scale=None):
    with Phase(nc, name) as ph:
        mean, var, dev = ph.sb("mean", [P, NB]), ph.sb("var", [P, NB]), ph.sb("dev", [P, NB])
        sq = ph.sb("sq", [P, NB, D])
        dv, va, sd, rows, stored = (ph.sem(n) for n in ("dv", "va", "sd", "rows", "stored"))
        block = ph.ctx.enter_context(nc.Block())
        wide = [P, NB, D]

        @block.vector
        def _(dve):
            v = nc.vector
            link = linker(dve, dv, Steps())
            link(v.tensor_reduce(mean[:, :], x[:, :, :], AX, ALU.add))
            link(v.tensor_scalar(mean[:, :], mean[:, :], 1.0 / D, None, ALU.mult))
            link(v.tensor_tensor(out[:, :, :], x[:, :, :], mean[:, :, None].to_broadcast(wide), ALU.subtract))
            link(v.tensor_tensor(sq[:, :, :], out[:, :, :], out[:, :, :], ALU.mult))
            link(v.tensor_reduce(var[:, :], sq[:, :, :], AX, ALU.add))
            v.tensor_scalar(var[:, :], var[:, :], 1.0 / D, EPS, ALU.mult, ALU.add).then_inc(va, 1)
            dve.wait_ge(sd, 1)
            link(v.reciprocal(dev[:, :], dev[:, :]))
            link(v.tensor_tensor(out[:, :, :], out[:, :, :], dev[:, :, None].to_broadcast(wide), ALU.mult))
            link(v.tensor_scalar(out[:, :, :], out[:, :, :], 0.0, None, ALU.max))
            if scale is None:
                v.tensor_copy(sq[:, :, :], out[:, :, :]).then_inc(rows, 1)
            else:
                v.tensor_tensor(sq[:, :, :], out[:, :, :], scale[:, :, None].to_broadcast(wide), ALU.mult).then_inc(rows, 1)

        @block.scalar
        def _(act):
            act.wait_ge(va, 1)
            nc.scalar.activation(dev[:, :], var[:, :], ACT.Sqrt).then_inc(sd, 1)

        @block.sync
        def _(sp):
            if table is not None:
                sp.wait_ge(rows, 1)
                sp.dma_start(table.rearrange("(p j) f -> p j f", p=P), sq[:, :, :]).then_inc(stored, 16)
                sp.wait_ge(stored, 16)


def store_rows(nc, name, table, rows, width):
    with Phase(nc, name) as ph:
        stored = ph.sem("stored")
        block = ph.ctx.enter_context(nc.Block())

        @block.sync
        def _(sp):
            sp.dma_start(table.rearrange("(p j) f -> p j f", p=P), rows[:, :, 0:width]).then_inc(stored, 16)
            sp.wait_ge(stored, 16)


def scatter_to_starts(nc, m, name, spread, rows, table, first):
    with Phase(nc, name) as ph:
        put, got = ph.sem("put"), ph.sem("got")
        block = ph.ctx.enter_context(nc.Block())

        @block.gpsimd
        def _(pool):
            pool.indirect_dma_start(out=first[:, :], out_offset=None, in_=table,
                                    in_offset=bass.IndirectOffsetOnAxis(ap=m["dst0"][:, 0:1], axis=0)).then_inc(got, 16)
            for j in range(NB):
                pool.indirect_dma_start(out=spread, out_offset=bass.IndirectOffsetOnAxis(ap=m["ixStart"][:, j:j + 1], axis=0),
                                        in_=rows(j), in_offset=None).then_inc(put, 16)
                pool.wait_ge(put, 16 * (j + 1))
            pool.wait_ge(got, 16)


def load_indices(sp, ix, src, ixin, free):
    srcv = src.rearrange("(p t) -> p t", p=P)
    with sp.Fori(0, ROUNDS) as i:
        for b in range(2):
            sp.wait_ge(free, i * 2 + b + 1)
            sp.dma_start(ix[:, b, :], srcv[:, bass.ds((i * 2 + b) * C, C)]).then_inc(ixin[b], 16)


def gather_rows(pool, ix, g, table, ixin, got, free, begun):
    with pool.Fori(0, ROUNDS) as i:
        for b in range(2):
            pool.wait_ge(free, i * 2 + b + 1)
            pool.wait_ge(ixin[b], i * 16 + 16)
            pool.sem_inc(begun, 1)
            for c in range(C):
                pool.indirect_dma_start(out=g[:, b, c, :], out_offset=None, in_=table,
                                        in_offset=bass.IndirectOffsetOnAxis(ap=ix[:, b, c:c + 1], axis=0)
                                        ).then_inc(got[b], 16)


def gather_pass(nc, m, name, table, src):
    with Phase(nc, name) as ph:
        ix = ph.sb("ix", [P, 2, C], I32)
        g = ph.sb("g", [P, 2, C, D])
        same = ph.sb("same", [P, D, S1])
        msg = ph.sb("msg", [P, D, S1])
        out = ph.sb("out", [P, D, S1])
        rows = ph.sb("rows", [P, C, D])
        free, begun, spread, scanned, packed, stored, zs, dv = (
            ph.sem(k) for k in ("free", "begun", "spread", "scanned", "packed", "stored", "zs", "dv"))
        ixin = [ph.sem(f"ixin{b}") for b in range(2)]
        got = [ph.sem(f"got{b}") for b in range(2)]
        block = ph.ctx.enter_context(nc.Block())
        scv = m["SC"][0:EP, :].rearrange("(p t) f -> p t f", p=P)

        @block.sync
        def _(sp):
            load_indices(sp, ix, src, ixin, free)

        @block.gpsimd
        def _(pool):
            gather_rows(pool, ix, g, table, ixin, got, free, begun)

        @block.scalar
        def _(act):
            act.sem_inc(free, 2)
            act.wait_ge(zs, 2)
            with act.Fori(0, ROUNDS) as i:
                for b in range(2):
                    nc.scalar.copy(same[:, :, 1:S1],
                                   m["same"][:, None, bass.ds((i * 2 + b) * C, C)].to_broadcast([P, D, C])).then_inc(spread, 1)
                    act.wait_ge(got[b], i * (16 * C) + 16 * C)
                    nc.scalar.copy(msg[:, :, 1:S1], g[:, b, :, :].rearrange("p c f -> p f c")).then_inc(free, 1)
                    act.wait_ge(scanned, i * 2 + b + 1)
                    nc.scalar.copy(rows[:, :, :], out[:, :, 1:S1].rearrange("p f c -> p c f")).then_inc(packed, 1)
                    act.wait_ge(packed, i * 2 + b + 1)
                    act.dma_start(scv[:, bass.ds((i * 2 + b) * C, C), :], rows[:, :, :]).then_inc(stored, 16)
                    act.wait_ge(stored, i * 32 + (b + 1) * 16)

        @block.vector
        def _(dve):
            v = nc.vector
            n = Steps()
            link = linker(dve, dv, n)
            v.memset(same[:, :, 0:1], 0.0).then_inc(zs, 1)
            v.memset(out[:, :, C:S1], 0.0).then_inc(zs, 1)
            dve.wait_ge(zs, 2)
            with dve.Fori(0, ROUNDS) as i:
                n.enter(i, 2)
                for b in range(2):
                    link(v.tensor_copy(msg[:, :, 0:1], out[:, :, C:S1]))
                    dve.wait_ge(free, i * 2 + b + 3)
                    dve.wait_ge(spread, i * 2 + b + 1)
                    v.tensor_tensor_scan(out[:, :, :].rearrange("p f c -> p (f c)"), same[:, :, :].rearrange("p f c -> p (f c)"),
                                         msg[:, :, :].rearrange("p f c -> p (f c)"), 0.0, ALU.mult, ALU.add).then_inc(scanned, 1)
                    dve.wait_ge(packed, i * 2 + b + 1)
            n.leave(ROUNDS)
            dve.wait_ge(scanned, CHUNKS)
            link(v.tensor_copy(m["last"][:, 0:D], out[:, :, C]))


def carry_and_collect(nc, m, name):
    W = D
    with Phase(nc, name) as ph:
        pad = ph.sb("pad", [P, 2, P])
        padT = ph.sb("padT", [P, 2, P])
        carT = ph.sb("carT", [P, P + 1])
        car = ph.sb("car", [P, P])
        part = ph.sb("part", [P, NB, D])
        none = ph.sb("none", [1, D])
        psT = ph.ps("psT", [P, 512])
        dv, ready, turned, scanned, back, cars, stored, zrow = (
            ph.sem(k) for k in ("dv", "ready", "turned", "scanned", "back", "cars", "stored", "zrow"))
        gotS, gotC = ph.sem("gotS"), ph.sem("gotC")
        block = ph.ctx.enter_context(nc.Block())

        @block.vector
        def _(dve):
            v = nc.vector
            link = linker(dve, dv, Steps())
            v.memset(none[:, :], 0.0).then_inc(zrow, 1)
            link(v.memset(pad[:, :, :], 0.0))
            link(v.memset(carT[:, :], 0.0))
            v.tensor_copy(pad[:, 0, 0:W], m["last"][:, 0:W]).then_inc(ready, 1)
            v.tensor_copy(pad[:, 1, 0:W], m["whole"][:, 0:1].to_broadcast([P, W])).then_inc(ready, 1)
            dve.wait_ge(turned, 2)
            link(v.tensor_copy(padT[:, :, :], psT[:, 0:2 * P].rearrange("p (k c) -> p k c", k=2)))
            v.tensor_tensor_scan(carT[:, 1:P + 1], padT[:, 1, :], padT[:, 0, :], 0.0, ALU.mult, ALU.add).then_inc(scanned, 1)
            dve.wait_ge(back, 1)
            v.tensor_copy(car[:, :], psT[:, 2 * P:3 * P]).then_inc(cars, 1)
            dve.wait_ge(gotS, 16 * NB)
            dve.wait_ge(gotC, 16 * NB)
            v.tensor_tensor(m["agg"][:, :, :], m["agg"][:, :, :], part[:, :, :], ALU.add).then_inc(dv, 1)

        @block.tensor
        def _(pe):
            pe.wait_ge(ready, 2)
            nc.tensor.transpose(psT[:, 0:P], pad[:, 0, :], m["ident"][:, :]).then_inc(turned, 1)
            nc.tensor.transpose(psT[:, P:2 * P], pad[:, 1, :], m["ident"][:, :]).then_inc(turned, 1)
            pe.wait_ge(scanned, 1)
            nc.tensor.transpose(psT[:, 2 * P:3 * P], carT[:, 0:P], m["ident"][:, :]).then_inc(back, 1)

        @block.sync
        def _(sp):
            sp.wait_ge(zrow, 1)
            sp.dma_start(m["CAR"][P:P + 1, :], none[:, :]).then_inc(stored, 16)
            sp.wait_ge(cars, 1)
            sp.dma_start(m["CAR"][0:P, :], car[:, 0:D]).then_inc(stored, 16)
            sp.wait_ge(stored, 32)

        @block.gpsimd
        def _(pool):
            for j in range(NB):
                pool.indirect_dma_start(out=m["agg"][:, j, :], out_offset=None, in_=m["SC"],
                                        in_offset=bass.IndirectOffsetOnAxis(ap=m["ixEnd"][:, j:j + 1], axis=0)).then_inc(gotS, 16)
            pool.wait_ge(stored, 32)
            for j in range(NB):
                pool.indirect_dma_start(out=part[:, j, :], out_offset=None, in_=m["CAR"],
                                        in_offset=bass.IndirectOffsetOnAxis(ap=m["ixCarry"][:, j:j + 1], axis=0)).then_inc(gotC, 16)


def expand_degrees(nc, m):
    with Phase(nc, "xd") as ph:
        ex = ph.sb("ex", [P, T])
        dv, loaded = ph.sem("dv"), ph.sem("loaded")
        block = ph.ctx.enter_context(nc.Block())

        @block.sync
        def _(sp):
            sp.dma_start(ex[:, :], m["EXD"][0:EP, :].rearrange("(p t) f -> p (t f)", p=P)).then_inc(loaded, 16)
            sp.wait_ge(loaded, 16)

        @block.vector
        def _(dve):
            link = linker(dve, dv, Steps())
            dve.wait_ge(loaded, 16)
            link(nc.vector.tensor_tensor_scan(m["wts"][:, :], m["same"][:, :], ex[:, :], m["firstd"][:, 0:1], ALU.mult, ALU.add))


def weighted_histogram(nc, m):
    with Phase(nc, "wh") as ph:
        keyp, keyj, kf = (ph.sb(k, [P, T]) for k in ("keyp", "keyj", "kf"))
        hotp = ph.sb("hotp", [P, 2, HG, P])
        hotj = ph.sb("hotj", [P, 2, HG, NB])
        hotw = ph.sb("hotw", [P, 2, HG, NB])
        zb = ph.sb("zb", [P, P])
        acc = ph.ps("acc", [P, 512])
        dv, hot, used, zs, done = (ph.sem(k) for k in ("dv", "hot", "used", "zs", "done"))
        block = ph.ctx.enter_context(nc.Block())

        @block.vector
        def _(dve):
            v = nc.vector
            n = Steps()
            link = linker(dve, dv, n)
            v.memset(zb[:, :], 0.0).then_inc(zs, 1)
            link(v.tensor_scalar(kf[:, :], m["srcf"][:, :], 1.0 / NB, 0.5 / NB - 0.5, ALU.mult, ALU.add))
            link(v.tensor_scalar(keyp[:, :], kf[:, :], MAGIC, -MAGIC, ALU.add, ALU.add))
            link(v.scalar_tensor_tensor(keyj[:, :], keyp[:, :], -float(NB), m["srcf"][:, :], ALU.mult, ALU.add))
            with dve.Fori(0, HGROUNDS) as i:
                n.enter(i, 2)
                for b in range(2):
                    dve.wait_ge(used, i * 2 + b + 1)
                    at = bass.ds((i * 2 + b) * HG, HG)
                    link(v.tensor_tensor(hotj[:, b, :, :], m["iota"][:, None, 0:NB].to_broadcast([P, HG, NB]),
                                         keyj[:, at][:, :, None].to_broadcast([P, HG, NB]), ALU.is_equal))
                    v.tensor_tensor(hotp[:, b, :, :], m["iota"][:, None, :].to_broadcast([P, HG, P]),
                                    keyp[:, at][:, :, None].to_broadcast([P, HG, P]), ALU.is_equal).then_inc(hot, 1)
                    v.tensor_tensor(hotw[:, b, :, :], hotj[:, b, :, :],
                                    m["wts"][:, at][:, :, None].to_broadcast([P, HG, NB]), ALU.mult).then_inc(hot, 1)
            n.leave(HGROUNDS)
            dve.wait_ge(done, 1)
            link(v.tensor_copy(m["tsum"][:, :], acc[:, 0:NB]))

        @block.tensor
        def _(pe):
            pe.wait_ge(zs, 1)
            nc.tensor.matmul(acc[:, 0:NB], zb[:, :], zb[:, 0:NB], start=True, stop=False).then_inc(used, 2)
            with pe.Fori(0, HGROUNDS) as i:
                for b in range(2):
                    pe.wait_ge(hot, i * 4 + b * 2 + 2)
                    for c in range(HG):
                        last = nc.tensor.matmul(acc[:, 0:NB], hotp[:, b, c, :], hotw[:, b, c, :], start=False, stop=False)
                    last.then_inc(used, 1)
            nc.tensor.matmul(acc[:, 0:NB], zb[:, :], zb[:, 0:NB], start=False, stop=True).then_inc(done, 1)


def hamilton_gradient(nc, m, a):
    with Phase(nc, "hg") as ph:
        w1b = ph.sb("w1b", [P, 4, P])
        w1 = ph.sb("w1", [D, P])
        jt = ph.sb("jt", [D, D])
        w2 = ph.sb("w2", [P, D])
        w2s = ph.sb("w2s", [P, 1])
        b1 = ph.sb("b1", [P, 1])
        rw = ph.sb("rw", [P, D])
        coef = ph.sb("coef", [P, NB])
        slot, slotT = ph.sb("slot", [P, 4 * D]), ph.sb("slotT", [P, P])
        th, sq, gr = (ph.sb(k, [P, 4 * P]) for k in ("th", "sq", "gr"))
        psT, psZ, psU, psW = (ph.ps(k, [P, 512]) for k in ("psT", "psZ", "psU", "psW"))
        names = ("dv", "zeroed", "loaded", "jw", "weights", "slotted", "turned", "flat", "hidden", "tanhed", "grads", "back")
        dv, zeroed, loaded, jw, weights, slotted, turned, flat, hidden, tanhed, grads, back = (ph.sem(k) for k in names)
        block = ph.ctx.enter_context(nc.Block())

        @block.sync
        def _(sp):
            sp.wait_ge(zeroed, 1)
            for b in range(4):
                sp.dma_start(w1b[D * b:D * b + D, b, :], a["W1"]).then_inc(loaded, 16)
            for dst, src in ((w1, "W1"), (jt, "JT"), (w2, "W2"), (b1, "b1")):
                sp.dma_start(dst[:, :], a[src]).then_inc(loaded, 16)
            sp.wait_ge(loaded, 128)

        @block.vector
        def _(dve):
            v = nc.vector
            n = Steps()
            link = linker(dve, dv, n)
            v.memset(w1b[:, :, :], 0.0).then_inc(zeroed, 1)
            link(v.tensor_tensor(coef[:, :], m["dinv"][:, :], m["tsum"][:, :], ALU.mult))
            dve.wait_ge(loaded, 128)
            link(v.tensor_reduce(w2s[:, :], w2[:, :], AX, ALU.add))
            dve.wait_ge(jw, 1)
            v.tensor_scalar(rw[:, :], psW[:, 0:D], w2s[:, 0:1], None, ALU.mult).then_inc(weights, 1)
            with dve.Fori(0, NG) as g:
                n.enter(g, 2)
                dve.wait_ge(tanhed, g + 1)
                link(v.tensor_tensor(sq[:, :], th[:, :], th[:, :], ALU.mult))
                v.tensor_scalar(gr[:, :], sq[:, :], -1.0, 1.0, ALU.mult, ALU.add).then_inc(grads, 1)
                dve.wait_ge(back, g + 1)
                link(v.tensor_tensor(m["H"][:, bass.ds(g * 4, 4), :], psU[:, 0:4 * D].rearrange("p (b f) -> p b f", b=4),
                                     coef[:, bass.ds(g * 4, 4)][:, :, None].to_broadcast([P, 4, D]), ALU.mult))
            n.leave(NG)

        @block.scalar
        def _(act):
            act.wait_ge(loaded, 128)
            with act.Fori(0, NG) as g:
                nc.scalar.copy(slot[:, :].rearrange("p (b f) -> p b f", b=4), m["agg"][:, bass.ds(g * 4, 4), :]).then_inc(slotted, 1)
                act.wait_ge(turned, g + 1)
                nc.scalar.copy(slotT[:, :], psT[:, 0:P]).then_inc(flat, 1)
                act.wait_ge(hidden, g + 1)
                nc.scalar.activation(th[:, :], psZ[:, :], ACT.Tanh, bias=b1[:, 0:1]).then_inc(tanhed, 1)

        @block.tensor
        def _(pe):
            pe.wait_ge(loaded, 128)
            nc.tensor.matmul(psW[:, 0:D], w1[:, :], jt[:, :], start=True, stop=True).then_inc(jw, 1)
            pe.wait_ge(weights, 1)
            with pe.Fori(0, NG) as g:
                pe.wait_ge(slotted, g + 1)
                nc.tensor.transpose(psT[:, 0:P], slot[:, :], m["ident"][:, :]).then_inc(turned, 1)
                pe.wait_ge(flat, g + 1)
                for b in range(4):
                    last = nc.tensor.matmul(psZ[:, b * P:(b + 1) * P], w1b[:, b, :], slotT[:, :], start=True, stop=True)
                last.then_inc(hidden, 1)
                pe.wait_ge(grads, g + 1)
                for b in range(4):
                    last = nc.tensor.matmul(psU[:, b * D:(b + 1) * D], gr[:, b * P:(b + 1) * P], rw[:, :], start=True, stop=True)
                last.then_inc(back, 1)


def scatter_pass(nc, m):
    Q, B4 = 4, C // 4
    with Phase(nc, "sc") as ph:
        ex = ph.sb("ex", [P, 2, C, D])
        same = ph.sb("same", [P, D, S1])
        msg = ph.sb("msg", [P, D, S1])
        val = ph.sb("val", [P, 2, D, S1])
        sid = ph.sb("sid", [P, 2, C])
        tos = ph.sb("tos", [P, 2, C])
        eq = ph.sb("eq", [P, 2, Q, P])
        earlier = ph.sb("earlier", [P, Q, P])
        dup = ph.sb("dup", [P, 3, Q])
        trash = ph.sb("trash", [P, 1])
        vals = ph.sb("vals", [P, 2, Q, D])
        ids = ph.sb("ids", [P, 2, Q], I32)
        psB = [ph.ps(f"psB{k}", [P, 512]) for k in range(2)]
        psV = [ph.ps(f"psV{k}", [P, 512]) for k in range(2)]
        names = ("dv", "zs", "taken", "spread", "msgs", "scanned", "named", "wide", "equal", "summed", "copied", "aimed", "go")
        dv, zs, taken, spread, msgs, scanned, named, wide, equal, summed, copied, aimed, go = (ph.sem(k) for k in names)
        exin = [ph.sem(f"exin{b}") for b in range(2)]
        chain = [ph.sem(f"chain{k}") for k in range(CHAINS)]
        block = ph.ctx.enter_context(nc.Block())
        exv = m["EX"][0:EP, :].rearrange("(p t) f -> p t f", p=P)

        @block.sync
        def _(sp):
            with sp.Fori(0, ROUNDS) as i:
                for b in range(2):
                    sp.wait_ge(taken, i * 2 + b + 1)
                    sp.dma_start(ex[:, b, :, :], exv[:, bass.ds((i * 2 + b) * C, C), :]).then_inc(exin[b], 16)

        @block.scalar
        def _(act):
            act.sem_inc(taken, 2)
            act.sem_inc(copied, 2)
            act.wait_ge(zs, 2)
            with act.Fori(0, ROUNDS) as i:
                for b in range(2):
                    nc.scalar.copy(same[:, :, 1:S1],
                                   m["same"][:, None, bass.ds((i * 2 + b) * C, C)].to_broadcast([P, D, C])).then_inc(spread, 1)
                    act.wait_ge(exin[b], i * 16 + 16)
                    nc.scalar.copy(msg[:, :, 1:S1], ex[:, b, :, :].rearrange("p c f -> p f c")).then_inc(taken, 1)
                    for q in range(B4):
                        lb = b * B4 + q
                        k = lb % 2
                        act.wait_ge(summed, i * (2 * B4) + lb + 3)
                        for r in range(Q):
                            act.wait_ge(chain[k * Q + r], i * (16 * B4) + 16 * (lb // 2 + 1))
                        nc.scalar.copy(vals[:, k, :, :], psV[k][:, 0:Q * D].rearrange("p (r f) -> p r f", r=Q)).then_inc(copied, 1)

        @block.vector
        def _(dve):
            v = nc.vector
            n = Steps()
            link = linker(dve, dv, n)
            v.memset(same[:, :, 0:1], 0.0).then_inc(zs, 1)
            v.tensor_copy(val[:, 1, :, C:S1], m["first"][:, :, None]).then_inc(zs, 1)
            dve.wait_ge(zs, 2)
            link(v.tensor_scalar(trash[:, :], m["rowid"][:, :], float(NP), None, ALU.add))
            with dve.Fori(0, ROUNDS) as i:
                n.enter(i, 2 * (1 + B4 * 4))
                for b in range(2):
                    at = bass.ds((i * 2 + b) * C, C)
                    v.tensor_copy(sid[:, b, :], m["srcf"][:, at]).then_inc(named, 1)
                    v.tensor_scalar(tos[:, b, :], m["srcf"][:, at], -1.0, trash[:, 0:1], ALU.mult, ALU.add).then_inc(named, 1)
                    link(v.tensor_copy(msg[:, :, 0:1], val[:, 1 - b, :, C:S1]))
                    dve.wait_ge(spread, i * 2 + b + 1)
                    dve.wait_ge(taken, i * 2 + b + 3)
                    v.tensor_tensor_scan(val[:, b, :, :].rearrange("p f c -> p (f c)"), same[:, :, :].rearrange("p f c -> p (f c)"),
                                         msg[:, :, :].rearrange("p f c -> p (f c)"), 0.0, ALU.mult, ALU.add).then_inc(scanned, 1)
                    dve.wait_ge(scanned, i * 2 + b + 1)
                    dve.wait_ge(named, i * 4 + b * 2 + 2)
                    for q in range(B4):
                        lb = b * B4 + q
                        k = lb % 2
                        c = q * Q
                        dve.wait_ge(wide, i * (2 * B4) + lb + 1)
                        dve.wait_ge(summed, i * (2 * B4) + lb + 1)
                        v.tensor_tensor(eq[:, k, :, :], psB[k][:, :].rearrange("p (r c) -> p r c", r=Q),
                                        sid[:, b, c:c + Q][:, :, None].to_broadcast([P, Q, P]), ALU.is_equal).then_inc(equal, 1)
                        dve.wait_ge(equal, i * (2 * B4) + lb + 1)
                        link(v.tensor_tensor(earlier[:, :, :], eq[:, k, :, :],
                                             m["below"][:, None, :].to_broadcast([P, Q, P]), ALU.mult))
                        link(v.tensor_reduce(dup[:, 0, :], earlier[:, :, :], AX, ALU.add))
                        link(v.tensor_scalar(dup[:, 1, :], dup[:, 0, :], 0.5, None, ALU.is_gt))
                        link(v.tensor_tensor(dup[:, 2, :], dup[:, 1, :], tos[:, b, c:c + Q], ALU.mult))
                        for r in range(Q):
                            dve.wait_ge(chain[k * Q + r], i * (16 * B4) + 16 * (lb // 2 + 1))
                        v.tensor_tensor(ids[:, k, :], dup[:, 2, :], sid[:, b, c:c + Q], ALU.add).then_inc(aimed, 1)
            n.leave(ROUNDS)

        @block.tensor
        def _(pe):
            pe.sem_inc(summed, 2)
            with pe.Fori(0, ROUNDS) as i:
                for b in range(2):
                    pe.wait_ge(named, i * 4 + b * 2 + 1)
                    for q in range(B4):
                        lb = b * B4 + q
                        k = lb % 2
                        c = q * Q
                        for r in range(Q):
                            last = nc.tensor.matmul(psB[k][:, r * P:(r + 1) * P], sid[:, b, c + r:c + r + 1].to_broadcast([P, P]),
                                                    m["ident"][:, :], start=True, stop=True)
                        last.then_inc(wide, 1)
                        pe.wait_ge(equal, i * (2 * B4) + lb + 1)
                        pe.wait_ge(copied, i * (2 * B4) + lb + 1)
                        for r in range(Q):
                            last = nc.tensor.matmul(psV[k][:, r * D:(r + 1) * D], eq[:, k, r, :], val[:, b, :, 1 + c + r],
                                                    start=True, stop=True)
                        last.then_inc(summed, 1)

        @block.gpsimd
        def _(pool):
            for k in range(CHAINS):
                pool.dma_start(m[f"ACC{k}"].rearrange("(p j) f -> p (j f)", p=P), m["zero"][:, :]).then_inc(chain[k], 16)
            with pool.Fori(0, ROUNDS) as i:
                for lb in range(2 * B4):
                    k = lb % 2
                    pool.wait_ge(copied, i * (2 * B4) + lb + 3)
                    pool.wait_ge(aimed, i * (2 * B4) + lb + 1)
                    pool.sem_inc(go, 1)
                    for r in range(Q):
                        pool.indirect_dma_start(out=m[f"ACC{k * Q + r}"], in_=vals[:, k, r, :], in_offset=None,
                                                out_offset=bass.IndirectOffsetOnAxis(ap=ids[:, k, r:r + 1], axis=0),
                                                compute_op=ALU.add).then_inc(chain[k * Q + r], 16)
            for k in range(CHAINS):
                pool.wait_ge(chain[k], 16 * (1 + T // CHAINS))


def add_gradient(nc, m):
    with Phase(nc, "ag") as ph:
        part = ph.sb("part", [P, 2, NB, D])
        dv, added = ph.sem("dv"), ph.sem("added")
        got = [ph.sem(f"got{b}") for b in range(2)]
        block = ph.ctx.enter_context(nc.Block())

        @block.sync
        def _(sp):
            for k in range(CHAINS):
                if k >= 2:
                    sp.wait_ge(added, k - 1)
                sp.dma_start(part[:, k % 2, :, :], m[f"ACC{k}"][0:NP, :].rearrange("(p j) f -> p j f", p=P)).then_inc(got[k % 2], 16)

        @block.vector
        def _(dve):
            link = linker(dve, dv, Steps())
            for k in range(CHAINS):
                dve.wait_ge(got[k % 2], 16 * (k // 2 + 1))
                if k == 0:
                    nc.vector.tensor_copy(m["agg"][:, :, :], part[:, 0, :, :]).then_inc(added, 1)
                else:
                    nc.vector.tensor_tensor(m["agg"][:, :, :], m["agg"][:, :, :], part[:, k % 2, :, :], ALU.add).then_inc(added, 1)
                dve.wait_ge(added, k + 1)
            link(nc.vector.tensor_tensor(m["agg"][:, :, :], m["agg"][:, :, :], m["dinv"][:, :, None].to_broadcast([P, NB, D]), ALU.mult))
            link(nc.vector.tensor_tensor(m["X"][:, :, :], m["X"][:, :, :], m["agg"][:, :, :], ALU.add))


def product_pass(nc, m, a):
    Q, B4 = 4, C // 4
    with Phase(nc, "pp") as ph:
        ix = ph.sb("ix", [P, 2, C], I32)
        g = ph.sb("g", [P, 2, C, D])
        ef = ph.sb("ef", [D, 2, C * P])
        sh = ph.sb("sh", [P, 2, C, 4])
        v1, c1, v2 = ph.sb("v1", [D, HID1]), ph.sb("c1", [HID1, 1]), ph.sb("v2", [HID1 + 1, WN])
        hid = ph.sb("hid", [HID1 + 1, 2, Q * P])
        ab = ph.sb("ab", [P, C, 16])
        vs = ph.sb("vs", [P, C, MUL, 3])
        vp = ph.sb("vp", [P, C, MUL * 3])
        p1 = ph.sb("p1", [P, Q, 128])
        p2 = ph.sb("p2", [P, 4, Q, 64])
        pq = ph.sb("pq", [P, 4, C, MUL])
        pm = ph.sb("pm", [P, C, MUL])
        same = ph.sb("same", [P, D, S1])
        msg = ph.sb("msg", [P, D, S1])
        out = ph.sb("out", [P, D, S1])
        rows = ph.sb("rows", [P, C, D])
        psH = [ph.ps(f"psH{k}", [P, 512]) for k in range(2)]
        psW = [ph.ps(f"psW{k}", [P, Q, WN]) for k in range(2)]
        names = ("free", "begun", "spread", "scanned", "packed", "stored", "zs", "dv", "weights", "ready", "hidden", "relued", "wide", "used")
        free, begun, spread, scanned, packed, stored, zs, dv, weights, ready, hidden, relued, wide, used = (ph.sem(k) for k in names)
        ixin = [ph.sem(f"ixin{b}") for b in range(2)]
        got = [ph.sem(f"got{b}") for b in range(2)]
        efin = [ph.sem(f"efin{b}") for b in range(2)]
        block = ph.ctx.enter_context(nc.Block())
        scv = m["SC"][0:EP, :].rearrange("(p t) f -> p t f", p=P)
        shv = a["sh"].rearrange("(p t) f -> p t f", p=P)
        srcv = a["src"].rearrange("(p t) -> p t", p=P)
        NBAT = 2 * B4

        @block.sync
        def _(sp):
            for dst, src in ((v1, "V1"), (c1, "c1"), (v2, "V2")):
                sp.dma_start(dst[:, :], a[src]).then_inc(weights, 16)
            with sp.Fori(0, ROUNDS) as i:
                for b in range(2):
                    at = bass.ds((i * 2 + b) * C, C)
                    sp.wait_ge(free, i * 2 + b + 1)
                    sp.dma_start(ix[:, b, :], srcv[:, at]).then_inc(ixin[b], 16)
                    sp.dma_start(sh[:, b, :, :], shv[:, at, :]).then_inc(efin[b], 16)
                    sp.dma_start(ef[:, b, :], a["efT"][:, bass.ds((i * 2 + b) * (C * P), C * P)]).then_inc(efin[b], 16)

        @block.gpsimd
        def _(pool):
            gather_rows(pool, ix, g, m["HT"], ixin, got, free, begun)

        @block.scalar
        def _(act):
            act.wait_ge(weights, 48)
            act.wait_ge(zs, 3)
            with act.Fori(0, ROUNDS) as i:
                for b in range(2):
                    nc.scalar.copy(same[:, :, 1:S1],
                                   m["same"][:, None, bass.ds((i * 2 + b) * C, C)].to_broadcast([P, D, C])).then_inc(spread, 1)
                    for q in range(B4):
                        lb = b * B4 + q
                        k = lb % 2
                        act.wait_ge(hidden, i * NBAT + lb + 1)
                        act.wait_ge(wide, i * NBAT + lb + 1)
                        nc.scalar.activation(hid[0:HID1, k, :], psH[k][0:HID1, :], ACT.Relu, bias=c1[:, 0:1]).then_inc(relued, 1)
                    act.wait_ge(scanned, i * 2 + b + 1)
                    nc.scalar.copy(rows[:, :, :], out[:, :, 1:S1].rearrange("p f c -> p c f")).then_inc(packed, 1)
                    act.wait_ge(packed, i * 2 + b + 1)
                    act.dma_start(scv[:, bass.ds((i * 2 + b) * C, C), :], rows[:, :, :]).then_inc(stored, 16)
                    act.wait_ge(stored, i * 32 + (b + 1) * 16)

        @block.tensor
        def _(pe):
            pe.sem_inc(wide, 2)
            pe.wait_ge(ready, 1)
            pe.wait_ge(zs, 3)
            with pe.Fori(0, ROUNDS) as i:
                for b in range(2):
                    pe.wait_ge(efin[b], i * 32 + 32)
                    for q in range(B4):
                        lb = b * B4 + q
                        k = lb % 2
                        nc.tensor.matmul(psH[k][0:HID1, :], v1[:, :], ef[:, b, q * Q * P:(q + 1) * Q * P],
                                         start=True, stop=True).then_inc(hidden, 1)
                        pe.wait_ge(relued, i * NBAT + lb + 1)
                        pe.wait_ge(used, i * NBAT + lb + 1)
                        for r in range(Q):
                            last = nc.tensor.matmul(psW[k][:, r, :], hid[:, k, r * P:(r + 1) * P], v2[:, :], start=True, stop=True)
                        last.then_inc(wide, 1)

        @block.vector
        def _(dve):
            v = nc.vector
            n = Steps()
            link = linker(dve, dv, n)
            dve.sem_inc(free, 2)
            dve.sem_inc(used, 2)
            v.memset(same[:, :, 0:1], 0.0).then_inc(zs, 1)
            v.memset(out[:, :, C:S1], 0.0).then_inc(zs, 1)
            v.memset(hid[HID1:HID1 + 1, :, :], 1.0).then_inc(zs, 1)
            dve.wait_ge(zs, 3)
            dve.wait_ge(weights, 48)
            pair = v2[:, 0:128].rearrange("k (o h i) -> k o h i", o=MUL, h=2)
            link(v.tensor_scalar(v2[:, :], v2[:, :], ALPHA, None, ALU.mult))
            v.tensor_scalar(pair[:, :, 1, :], pair[:, :, 1, :], C110, None, ALU.mult).then_inc(ready, 1)
            with dve.Fori(0, ROUNDS) as i:
                n.enter(i, 2 * (2 + 2 * B4 + 2 * 3 + 1))
                for b in range(2):
                    dve.wait_ge(got[b], i * (16 * C) + 16 * C)
                    dve.wait_ge(efin[b], i * 32 + 32)
                    s_, v_ = g[:, b, :, 0:MUL], g[:, b, :, MUL:D]
                    v.tensor_tensor(ab[:, :, 0:MUL], s_, sh[:, b, :, 0:1].to_broadcast([P, C, MUL]), ALU.mult)
                    v.tensor_tensor(vp[:, :, :], v_, sh[:, b, :, 0:1].to_broadcast([P, C, 3 * MUL]), ALU.mult)
                    link(v.tensor_tensor(vs[:, :, :, :], v_.rearrange("p c (i x) -> p c i x", x=3),
                                         sh[:, b, :, None, 1:4].to_broadcast([P, C, MUL, 3]), ALU.mult))
                    link(v.tensor_reduce(ab[:, :, MUL:16], vs[:, :, :, :], AX, ALU.add))
                    for q in range(B4):
                        lb = b * B4 + q
                        k = lb % 2
                        c = q * Q
                        shape = [P, Q, MUL, MUL]
                        dve.wait_ge(wide, i * NBAT + lb + 3)
                        v.tensor_tensor(p1[:, :, :].rearrange("p r (o j) -> p r o j", o=MUL),
                                        psW[k][:, :, 0:128].rearrange("p r (o j) -> p r o j", o=MUL),
                                        ab[:, c:c + Q, None, :].to_broadcast([P, Q, MUL, 16]), ALU.mult)
                        v.tensor_tensor(p2[:, 0, :, :].rearrange("p r (o j) -> p r o j", o=MUL),
                                        psW[k][:, :, 128:192].rearrange("p r (o j) -> p r o j", o=MUL),
                                        s_[:, c:c + Q, None, :].to_broadcast(shape), ALU.mult)
                        for x in range(3):
                            last = v.tensor_tensor(p2[:, 1 + x, :, :].rearrange("p r (o j) -> p r o j", o=MUL),
                                                   psW[k][:, :, 192:256].rearrange("p r (o j) -> p r o j", o=MUL),
                                                   vp[:, c:c + Q, None, x::3].to_broadcast(shape), ALU.mult)
                        last.then_inc(used, 1)
                        dve.wait_ge(used, i * NBAT + lb + 3)
                        link(v.tensor_reduce(msg[:, 0:MUL, 1 + c:1 + c + Q].rearrange("p o r -> p r o"),
                                             p1[:, :, :].rearrange("p r (o j) -> p r o j", o=MUL), AX, ALU.add))
                        link(v.tensor_reduce(pq[:, :, c:c + Q, :],
                                             p2[:, :, :, :].rearrange("p x r (o j) -> p x (r o) j", o=MUL), AX, ALU.add))
                    mv = msg[:, MUL:D, 1:S1].rearrange("p (o x) c -> p x c o", x=3)
                    for x in range(3):
                        link(v.tensor_tensor(pm[:, :, :], pq[:, 0, :, :],
                                             sh[:, b, :, 1 + x:2 + x].to_broadcast([P, C, MUL]), ALU.mult))
                        link(v.tensor_tensor(mv[:, x], pm[:, :, :], pq[:, 1 + x, :, :], ALU.add))
                    link(v.tensor_copy(msg[:, :, 0:1], out[:, :, C:S1]))
                    dve.wait_ge(spread, i * 2 + b + 1)
                    v.tensor_tensor_scan(out[:, :, :].rearrange("p f c -> p (f c)"), same[:, :, :].rearrange("p f c -> p (f c)"),
                                         msg[:, :, :].rearrange("p f c -> p (f c)"), 0.0, ALU.mult, ALU.add).then_inc(scanned, 1)
                    dve.wait_ge(scanned, i * 2 + b + 1)
                    dve.sem_inc(free, 1)
                    dve.wait_ge(packed, i * 2 + b + 1)
            n.leave(ROUNDS)
            link(v.tensor_copy(m["last"][:, 0:D], out[:, :, C]))


def dense(nc, m, name, terms, width, weight, finish, steps, extra=()):
    K = len(terms)
    with Phase(nc, name) as ph:
        wb = [ph.sb(f"wb{k}", [P, 4, width]) for k in range(K)]
        slot, slotT = ph.sb("slot", [P, K, 4 * D]), ph.sb("slotT", [P, K, P])
        psT, psO = ph.ps("psT", [P, 512]), ph.ps("psO", [P, 512])
        dv, zeroed, loaded, slotted, turned, flat, made = (
            ph.sem(k) for k in ("dv", "zeroed", "loaded", "slotted", "turned", "flat", "made"))
        count = [0]
        block = ph.ctx.enter_context(nc.Block())

        @block.sync
        def _(sp):
            sp.wait_ge(zeroed, K)
            for k in range(K):
                count[0] += weight(sp, k, wb[k], loaded)
            for dst, src in extra:
                sp.dma_start(dst, src).then_inc(loaded, 16)
                count[0] += 1
            sp.wait_ge(loaded, 16 * count[0])

        @block.scalar
        def _(act):
            with act.Fori(0, NG) as g:
                for k in range(K):
                    nc.scalar.copy(slot[:, k, :].rearrange("p (b f) -> p b f", b=4), terms[k][:, bass.ds(g * 4, 4), :]).then_inc(slotted, 1)
                act.wait_ge(turned, g + 1)
                nc.scalar.copy(slotT[:, :, :], psT[:, 0:K * P].rearrange("p (k c) -> p k c", k=K)).then_inc(flat, 1)

        @block.tensor
        def _(pe):
            pe.wait_ge(loaded, 16 * count[0])
            with pe.Fori(0, NG) as g:
                pe.wait_ge(slotted, g * K + K)
                for k in range(K):
                    last = nc.tensor.transpose(psT[:, k * P:(k + 1) * P], slot[:, k, :], m["ident"][:, :])
                last.then_inc(turned, 1)
                pe.wait_ge(flat, g + 1)
                pe.wait_ge(zeroed, g + K + 1)
                for k in range(K):
                    last = nc.tensor.matmul(psO[:, 0:4 * width], slotT[:, k, :], wb[k][:, :, :].rearrange("p b w -> p (b w)"),
                                            start=(k == 0), stop=(k == K - 1))
                last.then_inc(made, 1)

        @block.vector
        def _(dve):
            v = nc.vector
            n = Steps()
            link = linker(dve, dv, n)
            for k in range(K):
                v.memset(wb[k][:, :, :], 0.0).then_inc(zeroed, 1)
            dve.wait_ge(loaded, 16 * count[0])
            dve.sem_inc(zeroed, 1)
            with dve.Fori(0, NG) as g:
                n.enter(g, steps)
                dve.wait_ge(made, g + 1)
                finish(v, link, bass.ds(g * 4, 4), psO[:, 0:4 * width].rearrange("p (b w) -> p b w", b=4))
                dve.sem_inc(zeroed, 1)
            n.leave(NG)


def blocks_of(src):
    def weight(sp, k, wb, loaded):
        total = 0
        for piece, col in src[k]:
            for b in range(4):
                sp.dma_start(wb[D * b:D * b + D, b, col:col + piece.shape[1]], piece).then_inc(loaded, 16)
                total += 1
        return total
    return weight


def self_interaction(nc, m, a):
    def weight(sp, k, wb, loaded):
        for b in range(4):
            sp.dma_start(wb[D * b:D * b + MUL, b, 0:MUL], a["si0"]).then_inc(loaded, 16)
            for x in range(3):
                with nc.allow_non_contiguous_dma(reason="8 x 8 numbers"):
                    sp.dma_start(wb[D * b + MUL + x:D * b + D:3, b, MUL + x:D:3], a["si1"]).then_inc(loaded, 16)
        return 16

    def finish(v, link, at, ps):
        link(v.scalar_tensor_tensor(m["H"][:, at, :], ps, SI_SCALE, m["agg"][:, at, :], ALU.mult, ALU.add))
        link(v.tensor_tensor(m["X"][:, at, :], m["X"][:, at, :], m["H"][:, at, :], ALU.add))
    dense(nc, m, "si", [m["H"]], D, weight, finish, 2)


def mean_layer(nc, m, a):
    with Phase(nc, "ml") as ph:
        bias = ph.sb("bias", [P, 4, D])
        dv = ph.sem("dv")
        with nc.Block() as block:
            @block.vector
            def _(dve):
                nc.vector.tensor_tensor(m["agg"][:, :, :], m["agg"][:, :, :],
                                        m["cinv"][:, :, None].to_broadcast([P, NB, D]), ALU.mult).then_inc(dv, 1)

        def finish(v, link, at, ps):
            link(v.tensor_tensor(m["H"][:, at, :], ps, bias[:, :, :], ALU.add))
            link(v.scalar_tensor_tensor(m["X"][:, at, :], m["H"][:, at, :], 0.0, m["X"][:, at, :], ALU.max, ALU.add))
        extra = [(bias[:, b, :], a["bs"].to_broadcast([P, D])) for b in range(4)]
        dense(nc, m, "md", [m["H"], m["agg"]], D, blocks_of([[(a["Ws"][0:D, :], 0)], [(a["Ws"][D:2 * D, :], 0)]]), finish, 2, extra)


def attention_inputs(nc, m, a):
    with Phase(nc, "kv") as ph:
        kv = ph.sb("kv", [P, NB, 2 * D])

        def finish(v, link, at, ps):
            link(v.tensor_copy(m["agg"][:, at, :], ps[:, :, 0:D]))
            link(v.tensor_copy(kv[:, at, :], ps[:, :, D:3 * D]))
        dense(nc, m, "qd", [m["H"]], 3 * D, blocks_of([[(a["Wq"], 0), (a["Wk"], D), (a["Wv"], 2 * D)]]), finish, 2)
        store_rows(nc, "sq", m["QT"], m["agg"], D)
        store_rows(nc, "sk", m["KV"], kv, 2 * D)


def attention_pass(nc, m, a):
    W = D + 1
    with Phase(nc, "at") as ph:
        ix = ph.sb("ix", [P, 2, C], I32)
        g = ph.sb("g", [P, 2, C, 2 * D])
        ex = ph.sb("ex", [P, 2, C, D])
        same = ph.sb("same", [P, D, S1])
        qm = ph.sb("qm", [P, D, S1])
        qo = ph.sb("qo", [P, D, S1])
        prod = ph.sb("prod", [P, C, D])
        sc, neg, dl, sd, er, ew = (ph.sb(k, [P, C]) for k in ("sc", "neg", "dl", "sd", "er", "ew"))
        mx = ph.sb("mx", [P, S1])
        keep = ph.sb("keep", [P, W, S1])
        msg = ph.sb("msg", [P, W, S1])
        out = ph.sb("out", [P, W, S1])
        rows = ph.sb("rows", [P, C, W + 1])
        names = ("free", "begun", "spread", "queries", "scanned", "packed", "stored", "zs", "dv", "diffs", "exps")
        free, begun, spread, queries, scanned, packed, stored, zs, dv, diffs, exps = (ph.sem(k) for k in names)
        ixin = [ph.sem(f"ixin{b}") for b in range(2)]
        got = [ph.sem(f"got{b}") for b in range(2)]
        exin = [ph.sem(f"exin{b}") for b in range(2)]
        block = ph.ctx.enter_context(nc.Block())
        scv = m["SC34"][0:EP, :].rearrange("(p t) f -> p t f", p=P)
        exv = m["EX"][0:EP, :].rearrange("(p t) f -> p t f", p=P)
        srcv = a["src"].rearrange("(p t) -> p t", p=P)

        @block.sync
        def _(sp):
            with sp.Fori(0, ROUNDS) as i:
                for b in range(2):
                    at = bass.ds((i * 2 + b) * C, C)
                    sp.wait_ge(free, i * 2 + b + 1)
                    sp.dma_start(ix[:, b, :], srcv[:, at]).then_inc(ixin[b], 16)
                    sp.dma_start(ex[:, b, :, :], exv[:, at, :]).then_inc(exin[b], 16)

        @block.gpsimd
        def _(pool):
            gather_rows(pool, ix, g, m["KV"], ixin, got, free, begun)

        @block.scalar
        def _(act):
            act.wait_ge(zs, 5)
            with act.Fori(0, ROUNDS) as i:
                for b in range(2):
                    nc.scalar.copy(same[:, :, 1:S1],
                                   m["same"][:, None, bass.ds((i * 2 + b) * C, C)].to_broadcast([P, D, C])).then_inc(spread, 1)
                    act.wait_ge(exin[b], i * 16 + 16)
                    nc.scalar.copy(qm[:, :, 1:S1], ex[:, b, :, :].rearrange("p c f -> p f c")).then_inc(queries, 1)
                    act.wait_ge(diffs, i * 4 + b * 2 + 2)
                    nc.scalar.activation(er[:, :], dl[:, :], ACT.Exp).then_inc(exps, 1)
                    nc.scalar.activation(ew[:, :], sd[:, :], ACT.Exp).then_inc(exps, 1)
                    act.wait_ge(scanned, i * 4 + b * 2 + 2)
                    nc.scalar.copy(rows[:, :, 0:W], out[:, :, 1:S1].rearrange("p f c -> p c f")).then_inc(packed, 1)
                    nc.scalar.copy(rows[:, :, W:W + 1], mx[:, 1:S1][:, :, None]).then_inc(packed, 1)
                    act.wait_ge(packed, i * 4 + b * 2 + 2)
                    act.dma_start(scv[:, bass.ds((i * 2 + b) * C, C), :], rows[:, :, :]).then_inc(stored, 16)
                    act.wait_ge(stored, i * 32 + (b + 1) * 16)

        @block.vector
        def _(dve):
            v = nc.vector
            n = Steps()
            link = linker(dve, dv, n)
            dve.sem_inc(free, 2)
            v.memset(same[:, :, 0:1], 0.0).then_inc(zs, 1)
            v.memset(keep[:, :, 0:1], 0.0).then_inc(zs, 1)
            v.memset(out[:, :, C:S1], 0.0).then_inc(zs, 1)
            v.memset(mx[:, C:S1], -BIG).then_inc(zs, 1)
            v.tensor_copy(qo[:, :, C:S1], m["first"][:, :, None]).then_inc(zs, 1)
            dve.wait_ge(zs, 5)
            with dve.Fori(0, ROUNDS) as i:
                n.enter(i, 2 * 13)
                for b in range(2):
                    at = bass.ds((i * 2 + b) * C, C)
                    link(v.tensor_copy(qm[:, :, 0:1], qo[:, :, C:S1]))
                    dve.wait_ge(spread, i * 2 + b + 1)
                    dve.wait_ge(queries, i * 2 + b + 1)
                    v.tensor_tensor_scan(qo[:, :, :].rearrange("p f c -> p (f c)"), same[:, :, :].rearrange("p f c -> p (f c)"),
                                         qm[:, :, :].rearrange("p f c -> p (f c)"), 0.0, ALU.mult, ALU.add).then_inc(scanned, 1)
                    dve.wait_ge(scanned, i * 4 + b * 2 + 1)
                    dve.wait_ge(got[b], i * (16 * C) + 16 * C)
                    link(v.tensor_tensor(prod[:, :, :], qo[:, :, 1:S1].rearrange("p f c -> p c f"), g[:, b, :, 0:D], ALU.mult))
                    link(v.tensor_reduce(sc[:, :], prod[:, :, :], AX, ALU.add))
                    link(v.tensor_scalar(sc[:, :], sc[:, :], D ** -0.5, None, ALU.mult))
                    link(v.tensor_scalar(neg[:, :], m["same"][:, at], BIG, -BIG, ALU.mult, ALU.add))
                    link(v.tensor_copy(mx[:, 0:1], mx[:, C:S1]))
                    link(v.tensor_tensor_scan(mx[:, 1:S1], neg[:, :], sc[:, :], mx[:, 0:1], ALU.add, ALU.max))
                    link(v.tensor_tensor(dl[:, :], mx[:, 0:C], mx[:, 1:S1], ALU.subtract))
                    v.tensor_scalar(dl[:, :], dl[:, :], 0.0, None, ALU.min).then_inc(diffs, 1)
                    v.tensor_tensor(sd[:, :], sc[:, :], mx[:, 1:S1], ALU.subtract).then_inc(diffs, 1)
                    dve.wait_ge(exps, i * 4 + b * 2 + 2)
                    link(v.tensor_tensor(er[:, :], er[:, :], m["same"][:, at], ALU.mult))
                    link(v.tensor_copy(keep[:, :, 1:S1], er[:, None, :].to_broadcast([P, W, C])))
                    link(v.tensor_copy(msg[:, D:W, 1:S1], ew[:, None, :]))
                    link(v.tensor_tensor(msg[:, 0:D, 1:S1].rearrange("p f c -> p c f"), g[:, b, :, D:2 * D],
                                         ew[:, :, None].to_broadcast([P, C, D]), ALU.mult))
                    dve.sem_inc(free, 1)
                    link(v.tensor_copy(msg[:, :, 0:1], out[:, :, C:S1]))
                    v.tensor_tensor_scan(out[:, :, :].rearrange("p f c -> p (f c)"), keep[:, :, :].rearrange("p f c -> p (f c)"),
                                         msg[:, :, :].rearrange("p f c -> p (f c)"), 0.0, ALU.mult, ALU.add).then_inc(scanned, 1)
                    dve.wait_ge(scanned, i * 4 + b * 2 + 2)
                    dve.wait_ge(packed, i * 4 + b * 2 + 2)
            n.leave(ROUNDS)
            link(v.tensor_copy(m["last"][:, 0:W], out[:, :, C]))
            link(v.tensor_copy(m["last"][:, W:W + 1], mx[:, C:S1]))


def attention_collect(nc, m):
    W = D + 1
    with Phase(nc, "ac") as ph:
        pad = ph.sb("pad", [P, 3, P])
        padT = ph.sb("padT", [P, 3, P])
        neg, fa, fr = (ph.sb(k, [P, P]) for k in ("neg", "fa", "fr"))
        cm, ca = ph.sb("cm", [P, P + 1]), ph.sb("ca", [P, P + 1])
        car = ph.sb("car", [P, W + 1])
        none = ph.sb("none", [1, W + 1])
        ra, rb = ph.sb("ra", [P, NB, W + 1]), ph.sb("rb", [P, NB, W + 1])
        top, wa, wb = (ph.sb(k, [P, NB]) for k in ("top", "wa", "wb"))
        psT = ph.ps("psT", [P, 512])
        psC = ph.ps("psC", [P, 512])
        names = ("dv", "ready", "turned", "facin", "facs", "scanned", "back", "cars", "stored", "diffs", "exps")
        dv, ready, turned, facin, facs, scanned, back, cars, stored, diffs, exps = (ph.sem(k) for k in names)
        gotS, gotC = ph.sem("gotS"), ph.sem("gotC")
        block = ph.ctx.enter_context(nc.Block())

        @block.vector
        def _(dve):
            v = nc.vector
            link = linker(dve, dv, Steps())
            link(v.memset(pad[:, :, :], 0.0))
            link(v.memset(none[:, :], 0.0))
            link(v.memset(none[:, W:W + 1], -BIG))
            link(v.memset(ca[:, :], 0.0))
            link(v.memset(cm[:, :], -BIG))
            v.tensor_copy(pad[:, 0, 0:W], m["last"][:, 0:W]).then_inc(ready, 1)
            v.tensor_copy(pad[:, 1, 0:W], m["last"][:, W:W + 1].to_broadcast([P, W])).then_inc(ready, 1)
            v.tensor_copy(pad[:, 2, 0:W], m["whole"][:, 0:1].to_broadcast([P, W])).then_inc(ready, 1)
            dve.wait_ge(turned, 3)
            link(v.tensor_copy(padT[:, :, :], psT[:, 0:3 * P].rearrange("p (k c) -> p k c", k=3)))
            link(v.tensor_scalar(neg[:, :], padT[:, 2, :], BIG, -BIG, ALU.mult, ALU.add))
            link(v.tensor_tensor_scan(cm[:, 1:P + 1], neg[:, :], padT[:, 1, :], -BIG, ALU.add, ALU.max))
            v.tensor_tensor(fa[:, :], padT[:, 1, :], cm[:, 1:P + 1], ALU.subtract).then_inc(facin, 1)
            link(v.tensor_tensor(fr[:, :], cm[:, 0:P], cm[:, 1:P + 1], ALU.subtract))
            v.tensor_scalar(fr[:, :], fr[:, :], 0.0, None, ALU.min).then_inc(facin, 1)
            dve.wait_ge(facs, 2)
            link(v.tensor_tensor(fa[:, :], fa[:, :], padT[:, 0, :], ALU.mult))
            link(v.tensor_tensor(fr[:, :], fr[:, :], padT[:, 2, :], ALU.mult))
            v.tensor_tensor_scan(ca[:, 1:P + 1], fr[:, :], fa[:, :], 0.0, ALU.mult, ALU.add).then_inc(scanned, 1)
            dve.wait_ge(back, 2)
            v.tensor_copy(car[:, 0:W], psC[:, 0:W]).then_inc(cars, 1)
            v.tensor_copy(car[:, W:W + 1], psC[:, P:P + 1]).then_inc(cars, 1)
            dve.wait_ge(gotS, 16 * NB)
            dve.wait_ge(gotC, 16 * NB)
            link(v.tensor_tensor(top[:, :], ra[:, :, W], rb[:, :, W], ALU.max))
            v.tensor_tensor(wa[:, :], ra[:, :, W], top[:, :], ALU.subtract).then_inc(diffs, 1)
            v.tensor_tensor(wb[:, :], rb[:, :, W], top[:, :], ALU.subtract).then_inc(diffs, 1)
            dve.wait_ge(exps, 2)
            link(v.tensor_tensor(ra[:, :, 0:W], ra[:, :, 0:W], wa[:, :, None].to_broadcast([P, NB, W]), ALU.mult))
            link(v.tensor_tensor(rb[:, :, 0:W], rb[:, :, 0:W], wb[:, :, None].to_broadcast([P, NB, W]), ALU.mult))
            link(v.tensor_tensor(ra[:, :, 0:W], ra[:, :, 0:W], rb[:, :, 0:W], ALU.add))
            link(v.tensor_scalar(top[:, :], ra[:, :, D], 1e-6, None, ALU.add))
            link(v.reciprocal(top[:, :], top[:, :]))
            link(v.tensor_tensor(m["agg"][:, :, :], ra[:, :, 0:D], top[:, :, None].to_broadcast([P, NB, D]), ALU.mult))

        @block.scalar
        def _(act):
            act.wait_ge(facin, 2)
            nc.scalar.activation(fa[:, :], fa[:, :], ACT.Exp).then_inc(facs, 1)
            nc.scalar.activation(fr[:, :], fr[:, :], ACT.Exp).then_inc(facs, 1)
            act.wait_ge(diffs, 2)
            nc.scalar.activation(wa[:, :], wa[:, :], ACT.Exp).then_inc(exps, 1)
            nc.scalar.activation(wb[:, :], wb[:, :], ACT.Exp).then_inc(exps, 1)

        @block.tensor
        def _(pe):
            pe.wait_ge(ready, 3)
            for k in range(3):
                nc.tensor.transpose(psT[:, k * P:(k + 1) * P], pad[:, k, :], m["ident"][:, :]).then_inc(turned, 1)
            pe.wait_ge(scanned, 1)
            nc.tensor.transpose(psC[:, 0:P], ca[:, 0:P], m["ident"][:, :]).then_inc(back, 1)
            nc.tensor.transpose(psC[:, P:2 * P], cm[:, 0:P], m["ident"][:, :]).then_inc(back, 1)

        @block.sync
        def _(sp):
            sp.wait_ge(cars, 2)
            sp.dma_start(m["CAR34"][P:P + 1, :], none[:, :]).then_inc(stored, 16)
            sp.dma_start(m["CAR34"][0:P, :], car[:, :]).then_inc(stored, 16)
            sp.wait_ge(stored, 32)

        @block.gpsimd
        def _(pool):
            for j in range(NB):
                pool.indirect_dma_start(out=ra[:, j, :], out_offset=None, in_=m["SC34"],
                                        in_offset=bass.IndirectOffsetOnAxis(ap=m["ixEnd"][:, j:j + 1], axis=0)).then_inc(gotS, 16)
            pool.wait_ge(stored, 32)
            for j in range(NB):
                pool.indirect_dma_start(out=rb[:, j, :], out_offset=None, in_=m["CAR34"],
                                        in_offset=bass.IndirectOffsetOnAxis(ap=m["ixCarry"][:, j:j + 1], axis=0)).then_inc(gotC, 16)


def attention_output(nc, m, a):
    def finish(v, link, at, ps):
        link(v.tensor_tensor(m["H"][:, at, :], m["H"][:, at, :], ps, ALU.add))
        link(v.tensor_tensor(m["X"][:, at, :], m["X"][:, at, :], m["H"][:, at, :], ALU.add))
    dense(nc, m, "ao", [m["agg"]], D, blocks_of([[(a["Wo"], 0)]]), finish, 2)


def build(nc, a, out, stop=99):
    with ExitStack() as ctx:
        m = {}

        def sb(name, shape, dt=F32):
            m[name] = ctx.enter_context(nc.sbuf_tensor(name, shape, dt))

        def dram(name, shape):
            m[name] = nc.dram_tensor(name, shape, F32, kind="Internal").ap()
        for name in ("cnt", "deg", "dinv", "cinv", "tsum"):
            sb(name, [P, NB])
        for name in ("ixStart", "ixEnd", "ixCarry"):
            sb(name, [P, NB], I32)
        for name in ("iota", "ident", "below", "above"):
            sb(name, [P, P])
        sb("iotab", [P, P], BF16)
        sb("rowid", [P, 1])
        sb("dst0", [P, 1], I32)
        sb("whole", [P, 1])
        sb("last", [P, D + 2])
        sb("first", [P, D])
        sb("firstd", [P, 1])
        for name in ("X", "H", "agg"):
            sb(name, [P, NB, D])
        sb("same", [P, T])
        for name, width in (("HT", D), ("UT", D), ("QT", D), ("KV", 2 * D), ("DEG", 1)):
            dram(name, (NP, width))
        dram("SC", (EP + 1, D))
        dram("SC34", (EP + 1, D + 2))
        dram("EX", (EP + P, D))
        dram("EXD", (EP + P, 1))
        dram("CAR", (P + 1, D))
        dram("CAR34", (P + 1, D + 2))
        for k in range(CHAINS):
            dram(f"ACC{k}", (ACCROWS, D))
        body(nc, m, a, out)

def body(nc, m, a, out):
    with nc.sbuf_tensor("srcf", [P, T], F32) as m["srcf"], nc.sbuf_tensor("zero", [P, ZW], F32) as m["zero"]:
        with nc.sbuf_tensor("dstf", [P, T], F32) as m["dstf"]:
            load_edges(nc, m, a)
            histograms(nc, m)
        node_indices(nc, m, a)
        norm_relu(nc, m, "n0", m["X"], m["H"], m["HT"], m["dinv"])
        gather_pass(nc, m, "g0", m["HT"], a["src"])
        carry_and_collect(nc, m, "c0")
        with nc.sbuf_tensor("wts", [P, T], F32) as m["wts"]:
            scatter_to_starts(nc, m, "sd", m["EXD"], lambda j: m["deg"][:, j:j + 1], m["DEG"], m["firstd"])
            expand_degrees(nc, m)
            weighted_histogram(nc, m)
        hamilton_gradient(nc, m, a)
        store_rows(nc, "su", m["UT"], m["H"], D)
        scatter_to_starts(nc, m, "sx", m["EX"], lambda j: m["H"][:, j, :], m["UT"], m["first"])
        scatter_pass(nc, m)
        add_gradient(nc, m)
    norm_relu(nc, m, "n1", m["X"], m["H"], m["HT"])
    product_pass(nc, m, a)
    carry_and_collect(nc, m, "c1")
    self_interaction(nc, m, a)
    norm_relu(nc, m, "n2", m["X"], m["H"], m["HT"])
    gather_pass(nc, m, "g2", m["HT"], a["src"])
    carry_and_collect(nc, m, "c2")
    mean_layer(nc, m, a)
    norm_relu(nc, m, "n3", m["X"], m["H"], None)
    attention_inputs(nc, m, a)
    scatter_to_starts(nc, m, "sy", m["EX"], lambda j: m["agg"][:, j, :], m["QT"], m["first"])
    attention_pass(nc, m, a)
    attention_collect(nc, m)
    attention_output(nc, m, a)
    store_rows(nc, "st", out, m["X"], D)


def kernel(**inputs):
    import numpy as np
    import concourse.bacc as bacc
    from concourse.bass_utils import run_bass_kernel_spmd

    f = {k: np.asarray(v) for k, v in inputs.items()}
    arrays = {
        "x": np.concatenate([f["x"], np.zeros((NP - N, D), np.float32)]),
        "src": np.concatenate([f["src"], np.full(EP - E, NP - 1, np.int32)]),
        "dst": np.concatenate([np.full(1, NP, np.int32), f["dst"], np.full(EP - E, NP - 1, np.int32)]),
    }
    sh = np.concatenate([f["edge_attr_4"], np.zeros((EP - E, 4), np.float32)])
    arrays["sh"] = np.ascontiguousarray(sh)
    ef = np.concatenate([f["edge_attr_32"], np.zeros((EP - E, D), np.float32)])
    arrays["efT"] = np.ascontiguousarray(ef.reshape(P, T, D).transpose(2, 1, 0).reshape(D, T * P))
    arrays["W1"] = f["L0_gnn_W1"]
    arrays["b1"] = f["L0_gnn_b1"].reshape(P, 1)
    arrays["W2"] = f["L0_gnn_W2"]
    arrays["JT"] = np.ascontiguousarray(f["L0_gnn_J"].T)
    arrays["V1"] = f["L1_gnn_W1"]
    arrays["c1"] = f["L1_gnn_b1"].reshape(HID1, 1)
    w2 = np.concatenate([f["L1_gnn_W2"], f["L1_gnn_b2"].reshape(1, WN)]).reshape(HID1 + 1, 4, MUL, MUL)
    w2 = w2.transpose(0, 1, 3, 2)
    pair = np.stack([w2[:, 0], w2[:, 3]], axis=2).reshape(HID1 + 1, 128)
    arrays["V2"] = np.concatenate([pair, w2[:, 1].reshape(HID1 + 1, 64), w2[:, 2].reshape(HID1 + 1, 64)], axis=1)
    arrays["si0"] = f["L1_gnn_si_w0"]
    arrays["si1"] = f["L1_gnn_si_w1"]
    arrays["Ws"] = f["L2_gnn_W"]
    arrays["bs"] = f["L2_gnn_b"].reshape(1, D)
    arrays["Wq"], arrays["Wk"] = f["L3_gnn_Wq"], f["L3_gnn_Wk"]
    arrays["Wv"], arrays["Wo"] = f["L3_gnn_Wv"], f["L3_gnn_Wo"]

    nc = bacc.Bacc("TRN2", target_bir_lowering=False, num_devices=1)
    arrays = {k: np.ascontiguousarray(v) for k, v in arrays.items()}
    a = {k: nc.dram_tensor(f"in_{k}", v.shape, mybir.dt.from_np(v.dtype), kind="ExternalInput").ap()
         for k, v in arrays.items()}
    out = nc.dram_tensor("out", (NP, D), F32, kind="ExternalOutput").ap()
    build(nc, a, out)
    r = run_bass_kernel_spmd(nc, [{f"in_{k}": v for k, v in arrays.items()}], core_ids=[0])
    return r.results[0]["out"][0:N]
```

```python
from contextlib import ExitStack

import concourse.bass as bass
import concourse.mybir as mybir

F32 = mybir.dt.float32
BF16 = mybir.dt.bfloat16
I32 = mybir.dt.int32
ALU = mybir.AluOpType
ACT = mybir.ActivationFunctionType
AX = mybir.AxisListType.X

P = 128
D = 32
N = 12500
NB = 100
NP = P * NB
E = 412500
C = 52
T = 3224
CHUNKS = T // C
ROUNDS = CHUNKS // 2
JROUNDS = 13
JC = T // (2 * JROUNDS)
JG = 4
JN = JC // JG
EP = P * T
S1 = C + 1
HG = 13
HGROUNDS = T // (2 * HG)
HA = 4
CHAINS = 8
NG = NB // 4
ACCROWS = NP + P
ZW = ACCROWS * D // P
EPS = 1e-5
BIG = 1e30
MAGIC = 1.5 * 2 ** 23
MUL, HID1, WN = 8, 64, 256
ALPHA, C110, SI_SCALE = 0.25, 3.0 ** -0.5, 8.0 ** -0.5
assert T == JROUNDS * 2 * JN * JG and T % C == 0 and CHUNKS % 2 == 0 and T % (2 * HG) == 0 and C % 4 == 0 and EP >= E and ZW >= T


class Steps:

    def __init__(self):
        self.base, self.k, self.i, self.per = 0, 0, None, 0

    def enter(self, i, per):
        self.base, self.k, self.i, self.per = self.base + self.k, 0, i, per

    def leave(self, rounds):
        assert self.k == self.per, (self.k, self.per)
        self.base, self.k, self.i = self.base + rounds * self.per, 0, None

    def next(self):
        self.k += 1
        return self.base + self.k if self.i is None else self.i * self.per + (self.base + self.k)


def linker(eng, sem, steps):
    def link(ins):
        ins.then_inc(sem, 1)
        eng.wait_ge(sem, steps.next())
    return link


class Phase:

    def __init__(self, nc, name):
        self.nc, self.name, self.ctx, self.sems = nc, name, ExitStack(), []

    def __enter__(self):
        self.ctx.__enter__()
        return self

    def __exit__(self, *a):
        self.ctx.__exit__(*a)
        self.nc.clear_and_free_semaphores(self.sems)
        self.nc.all_engine_barrier()

    def sb(self, name, shape, dt=F32):
        return self.ctx.enter_context(self.nc.sbuf_tensor(f"{self.name}_{name}", shape, dt))

    def ps(self, name, shape, dt=F32):
        return self.ctx.enter_context(self.nc.psum_tensor(f"{self.name}_{name}", shape, dt))

    def sem(self, name):
        self.sems.append(self.nc.alloc_semaphore(f"{self.name}_{name}"))
        return self.sems[-1]


def cols(ap, i, n):
    return ap[:, bass.ds(i, n)]


def constants(nc, m):
    with Phase(nc, "co") as ph:
        consts, ready = ph.sem("consts"), ph.sem("ready")
        block = ph.ctx.enter_context(nc.Block())

        @block.gpsimd
        def _(pool):
            pool.iota(m["iota"][:, :], pattern=[[1, P]], base=0, channel_multiplier=0,
                      allow_small_or_imprecise_dtypes=True).then_inc(consts, 1)
            pool.iota(m["rowid"][:, :], pattern=[[0, 1]], base=0, channel_multiplier=1,
                      allow_small_or_imprecise_dtypes=True).then_inc(consts, 1)

        @block.vector
        def _(dve):
            v = nc.vector
            v.memset(m["zero"][:, :], 0.0).then_inc(ready, 1)
            dve.wait_ge(consts, 2)
            v.tensor_copy(m["iotab"][:, :], m["iota"][:, :]).then_inc(ready, 1)
            v.tensor_scalar(m["ident"][:, :], m["iota"][:, :], m["rowid"][:, 0:1], None, ALU.is_equal).then_inc(ready, 1)
            v.tensor_scalar(m["below"][:, :], m["iota"][:, :], m["rowid"][:, 0:1], None, ALU.is_lt).then_inc(ready, 1)
            v.tensor_scalar(m["above"][:, :], m["iota"][:, :], m["rowid"][:, 0:1], None, ALU.is_gt).then_inc(ready, 1)
            dve.wait_ge(ready, 5)


def check_order(nc, m, a):
    with Phase(nc, "ck") as ph:
        ids = ph.sb("ids", [P, 2, T], I32)
        less = ph.sb("less", [P, T])
        bad = ph.sb("bad", [P, 1])
        ones = ph.sb("ones", [P, 1])
        anyb = ph.sb("anyb", [1, 1])
        total = ph.ps("total", [P, 512])
        landed, dv, found, summed = (ph.sem(k) for k in ("landed", "dv", "found", "summed"))
        block = ph.ctx.enter_context(nc.Block())

        @block.sync
        def _(sp):
            for k in range(2):
                sp.dma_start(ids[:, k, :], a["dst"][k:k + EP].rearrange("(p t) -> p t", p=P)).then_inc(landed, 16)

        @block.vector
        def _(dve):
            v = nc.vector
            link = linker(dve, dv, Steps())
            link(v.memset(ones[:, :], 1.0))
            dve.wait_ge(landed, 32)
            link(v.tensor_tensor(less[:, :], ids[:, 0, :], ids[:, 1, :], ALU.is_gt))
            v.tensor_reduce(bad[:, :], less[:, :], AX, ALU.max).then_inc(found, 1)
            dve.wait_ge(summed, 1)
            link(v.tensor_scalar(anyb[:, :], total[0:1, 0:1], 0.5, None, ALU.is_gt))
            link(v.tensor_copy(m["flag"][:, :], anyb[:, :]))

        @block.tensor
        def _(pe):
            pe.wait_ge(found, 1)
            nc.tensor.matmul(total[0:1, 0:1], bad[:, :], ones[:, :], start=True, stop=True).then_inc(summed, 1)


def copy_ids(nc, m, a):
    with Phase(nc, "ci") as ph:
        copied = ph.sem("copied")
        block = ph.ctx.enter_context(nc.Block())

        @block.sync
        def _(sp):
            sp.dma_start(m["src"].rearrange("(p t) -> p t", p=P), a["src"].rearrange("(p t) -> p t", p=P)).then_inc(copied, 16)
            sp.dma_start(m["dst"][1:1 + EP].rearrange("(p t) -> p t", p=P),
                         a["dst"][1:1 + EP].rearrange("(p t) -> p t", p=P)).then_inc(copied, 16)
            sp.wait_ge(copied, 32)


def place_edges(nc, m, a):
    W = 4 + D
    with Phase(nc, "pl") as ph:
        free = ph.sb("free", [P, NB])
        dcol, scol = ph.sb("dcol", [P, 1]), ph.sb("scol", [P, 1])
        dix = ph.sb("dix", [P, 1], I32)
        eq, tri = ph.sb("eq", [P, P]), ph.sb("tri", [P, 2, P])
        cnt = ph.sb("cnt", [P, 2])
        base, pos, move, aim, trash = (ph.sb(k, [P, 1]) for k in ("base", "pos", "move", "aim", "trash"))
        place, baseix = ph.sb("place", [P, 1], I32), ph.sb("baseix", [P, 1], I32)
        rec = ph.sb("rec", [P, W + 2])
        bc = ph.ps("bc", [P, 512])
        names = ("dv", "begun", "stored", "loaded", "named", "wide", "read", "aimed", "moved", "put", "go")
        dv, begun, stored, loaded, named, wide, read, aimed, moved, put, go = (ph.sem(k) for k in names)
        block = ph.ctx.enter_context(nc.Block())
        erow = a["erow"].rearrange("(p t) f -> p t f", p=P)

        @block.sync
        def _(sp):
            sp.wait_ge(begun, 1)
            sp.dma_start(m["BASE"][0:NP, :].rearrange("(p j) f -> p (j f)", p=P), free[:, :]).then_inc(stored, 16)
            with sp.Fori(0, T) as t:
                sp.wait_ge(put, t * 16 + 16)
                sp.dma_start(rec[:, 0:W], erow[:, bass.ds(t, 1), :].rearrange("p t f -> p (t f)")).then_inc(loaded, 16)

        @block.vector
        def _(dve):
            v = nc.vector
            n = Steps()
            link = linker(dve, dv, n)
            v.tensor_copy(free[:, :], m["ixStart"][:, :]).then_inc(begun, 1)
            link(v.tensor_scalar(trash[:, :], m["rowid"][:, :], float(NP), None, ALU.add))
            with dve.Fori(0, T) as t:
                n.enter(t, 11)
                dve.wait_ge(put, t * 16 + 16)
                link(v.tensor_copy(dcol[:, :], m["dstf"][:, bass.ds(t, 1)]))
                v.tensor_copy(dix[:, :], dcol[:, :]).then_inc(named, 1)
                dve.wait_ge(wide, t + 1)
                link(v.tensor_scalar(eq[:, :], bc[:, 0:P], dcol[:, 0:1], None, ALU.is_equal))
                link(v.tensor_tensor(tri[:, 0, :], eq[:, :], m["below"][:, :], ALU.mult))
                link(v.tensor_tensor(tri[:, 1, :], eq[:, :], m["above"][:, :], ALU.mult))
                link(v.tensor_reduce(cnt[:, :], tri[:, :, :], AX, ALU.add))
                dve.wait_ge(read, t * 16 + 16)
                link(v.tensor_tensor(pos[:, :], base[:, :], cnt[:, 0:1], ALU.add))
                link(v.tensor_scalar(move[:, :], pos[:, :], 1.0, None, ALU.add))
                link(v.tensor_copy(place[:, :], pos[:, :]))
                link(v.tensor_scalar(cnt[:, 1:2], cnt[:, 1:2], 0.5, None, ALU.is_gt))
                link(v.tensor_tensor(aim[:, :], trash[:, :], dcol[:, :], ALU.subtract))
                link(v.scalar_tensor_tensor(baseix[:, :], aim[:, :], cnt[:, 1:2], dcol[:, :], ALU.mult, ALU.add))
                dve.wait_ge(loaded, t * 16 + 16)
                v.tensor_copy(rec[:, W:W + 1], m["srcf"][:, bass.ds(t, 1)]).then_inc(aimed, 1)
                v.tensor_copy(rec[:, W + 1:W + 2], dcol[:, :]).then_inc(aimed, 1)
            n.leave(T)

        @block.tensor
        def _(pe):
            with pe.Fori(0, T) as t:
                pe.wait_ge(named, t + 1)
                nc.tensor.matmul(bc[:, 0:P], dcol[:, 0:1].to_broadcast([P, P]), m["ident"][:, :], start=True, stop=True).then_inc(wide, 1)

        @block.gpsimd
        def _(pool):
            pool.wait_ge(stored, 16)
            pool.dma_start(m["BASE"][NP:NP + P, :], m["zero"][:, 0:1]).then_inc(put, 16)
            with pool.Fori(0, T) as t:
                pool.wait_ge(named, t + 1)
                pool.sem_inc(go, 1)
                pool.indirect_dma_start(out=base[:, :], out_offset=None, in_=m["BASE"],
                                        in_offset=bass.IndirectOffsetOnAxis(ap=dix[:, 0:1], axis=0)).then_inc(read, 16)
                pool.wait_ge(aimed, t * 2 + 2)
                pool.sem_inc(go, 1)
                pool.indirect_dma_start(out=m["BASE"], out_offset=bass.IndirectOffsetOnAxis(ap=baseix[:, 0:1], axis=0),
                                        in_=move[:, :], in_offset=None).then_inc(moved, 16)
                pool.wait_ge(moved, t * 16 + 16)
                pool.sem_inc(go, 1)
                pool.indirect_dma_start(out=m["REC"], out_offset=bass.IndirectOffsetOnAxis(ap=place[:, 0:1], axis=0),
                                        in_=rec[:, :], in_offset=None).then_inc(put, 16)
            pool.wait_ge(put, 16 * (T + 1))


def unpack_edges(nc, m, a):
    W, B4 = 4 + D, C // 4
    with Phase(nc, "un") as ph:
        rec = ph.sb("rec", [P, C, W + 2])
        ids = ph.sb("ids", [P, 2, C], I32)
        sh = ph.sb("sh", [P, C, 4])
        flat = ph.sb("flat", [P, C, D])
        efT = ph.sb("efT", [P, B4, P])
        ps = [ph.ps(f"ps{k}", [P, 512]) for k in range(2)]
        loaded, picked, turned, kept, stored, dv = (ph.sem(k) for k in ("loaded", "picked", "turned", "kept", "stored", "dv"))
        block = ph.ctx.enter_context(nc.Block())
        recv = m["REC"].rearrange("(p t) f -> p t f", p=P)
        srcv = m["src"].rearrange("(p t) -> p t", p=P)
        dstv = m["dst"][1:1 + EP].rearrange("(p t) -> p t", p=P)
        shv = m["sh"].rearrange("(p t) f -> p t f", p=P)

        @block.sync
        def _(sp):
            sp.sem_inc(stored, 64)
            with sp.Fori(0, CHUNKS) as i:
                sp.wait_ge(stored, i * 64 + 64)
                sp.dma_start(rec[:, :, :], recv[:, bass.ds(i * C, C), :]).then_inc(loaded, 16)
                sp.wait_ge(kept, i * B4 + B4)
                sp.dma_start(m["efT"][:, bass.ds(i * (B4 * P), B4 * P)], efT[:, :, :].rearrange("p q c -> p (q c)")).then_inc(stored, 16)
                sp.dma_start(srcv[:, bass.ds(i * C, C)], ids[:, 0, :]).then_inc(stored, 16)
                sp.dma_start(dstv[:, bass.ds(i * C, C)], ids[:, 1, :]).then_inc(stored, 16)
                sp.dma_start(shv[:, bass.ds(i * C, C), :], sh[:, :, :]).then_inc(stored, 16)
            sp.wait_ge(stored, CHUNKS * 64 + 64)

        @block.vector
        def _(dve):
            v = nc.vector
            with dve.Fori(0, CHUNKS) as i:
                dve.wait_ge(loaded, i * 16 + 16)
                v.tensor_copy(flat[:, :, :], rec[:, :, 4:W]).then_inc(picked, 1)
                v.tensor_copy(sh[:, :, :], rec[:, :, 0:4]).then_inc(picked, 1)
                v.tensor_copy(ids[:, 0, :], rec[:, :, W]).then_inc(picked, 1)
                v.tensor_copy(ids[:, 1, :], rec[:, :, W + 1]).then_inc(picked, 1)
                for q in range(B4):
                    dve.wait_ge(turned, i * B4 + q + 1)
                    v.tensor_copy(efT[:, q, :], ps[q % 2][:, 0:P]).then_inc(kept, 1)

        @block.tensor
        def _(pe):
            with pe.Fori(0, CHUNKS) as i:
                pe.wait_ge(picked, i * 4 + 4)
                for q in range(B4):
                    if q >= 2:
                        pe.wait_ge(kept, i * B4 + q - 1)
                    nc.tensor.transpose(ps[q % 2][:, 0:P], flat[:, 4 * q:4 * q + 4, :].rearrange("p r f -> p (r f)"),
                                        m["ident"][:, :]).then_inc(turned, 1)


def load_edges(nc, m, name, src, dst):
    with Phase(nc, name) as ph:
        ids = ph.sb("ids", [P, 3, T], I32)
        nxt = ph.sb("nxt", [P, 1], I32)
        w = {k: ph.sb(k, [P, 1]) for k in ("nf", "run", "part", "open", "row", "no")}
        before = ph.sb("before", [P, T])
        landed, ready, dv = (ph.sem(n) for n in ("landed", "ready", "dv"))
        block = ph.ctx.enter_context(nc.Block())

        @block.sync
        def _(sp):
            sp.dma_start(ids[:, 0, :], dst[1:1 + EP].rearrange("(p t) -> p t", p=P)).then_inc(landed, 16)
            sp.dma_start(ids[:, 1, :], dst[0:EP].rearrange("(p t) -> p t", p=P)).then_inc(landed, 16)
            sp.dma_start(ids[:, 2, :], src.rearrange("(p t) -> p t", p=P)).then_inc(landed, 16)
            with nc.allow_non_contiguous_dma(reason="one id per partition"):
                sp.dma_start(nxt[:, :], dst[1 + T:1 + T + EP].rearrange("(p t) -> p t", p=P)[:, 0:1]).then_inc(landed, 16)
            sp.wait_ge(landed, 64)

        @block.vector
        def _(dve):
            n = Steps()
            link = linker(dve, dv, n)
            dve.wait_ge(landed, 64)
            nc.vector.tensor_copy(m["dst0"][:, :], ids[:, 0, 0:1])
            nc.vector.tensor_copy(m["dstf"][:, :], ids[:, 0, :]).then_inc(ready, 1)
            link(nc.vector.tensor_copy(before[:, :], ids[:, 1, :]))
            nc.vector.tensor_copy(m["srcf"][:, :], ids[:, 2, :]).then_inc(ready, 1)
            dve.wait_ge(ready, 2)
            link(nc.vector.tensor_tensor(m["same"][:, :], m["dstf"][:, :], before[:, :], ALU.is_equal))
            link(nc.vector.tensor_reduce(m["whole"][:, :], m["same"][:, :], AX, ALU.min))
            v = nc.vector
            link(v.tensor_scalar(before[:, :], m["dstf"][:, :], m["dstf"][:, 0:1], None, ALU.is_equal))
            link(v.tensor_reduce(w["run"][:, :], before[:, :], AX, ALU.add))
            link(v.tensor_copy(w["nf"][:, :], nxt[:, :]))
            link(v.tensor_tensor(w["open"][:, :], w["nf"][:, :], m["dstf"][:, T - 1:T], ALU.not_equal))
            link(v.tensor_scalar(w["part"][:, :], w["run"][:, :], float(T), None, ALU.is_lt))
            link(v.tensor_tensor(w["open"][:, :], w["open"][:, :], w["part"][:, :], ALU.max))
            link(v.tensor_tensor(w["open"][:, :], w["open"][:, :], m["same"][:, 0:1], ALU.mult))
            link(v.scalar_tensor_tensor(w["row"][:, :], m["rowid"][:, :], float(T), w["run"][:, :], ALU.mult, ALU.add))
            link(v.tensor_scalar(w["no"][:, :], m["rowid"][:, :], float(EP + 1), None, ALU.add))
            link(v.scalar_tensor_tensor(w["row"][:, :], w["row"][:, :], -1.0, w["no"][:, :], ALU.add, ALU.subtract))
            link(v.tensor_tensor(w["row"][:, :], w["row"][:, :], w["open"][:, :], ALU.mult))
            link(v.tensor_tensor(m["ixPatch"][:, :], w["row"][:, :], w["no"][:, :], ALU.add))


def histogram(nc, m, name, key, result, *sync_work):
    with Phase(nc, name) as ph:
        keyp, keyj = ph.sb("keyp", [P, T], BF16), ph.sb("keyj", [P, T], BF16)
        kf, kg = ph.sb("kf", [P, T]), ph.sb("kg", [P, T])
        hotp = ph.sb("hotp", [P, 2, HG, P], BF16)
        hotj = ph.sb("hotj", [P, 2, HG, NB], BF16)
        far = ph.sb("far", [P, 2, HA, P], BF16)
        zb = ph.sb("zb", [P, P], BF16)
        acc = ph.ps("acc", [P, 512])
        dv, hot, used, zs, done, keyed, squared, hot_act = (
            ph.sem(n) for n in ("dv", "hot", "used", "zs", "done", "keyed", "squared", "hotact"))
        moved = [ph.sem(f"moved{k}") for k in range(len(sync_work))]
        block = ph.ctx.enter_context(nc.Block())

        @block.scalar
        def _(act):
            act.wait_ge(keyed, 1)
            with act.Fori(0, HGROUNDS) as i:
                for b in range(2):
                    act.wait_ge(used, i * 2 + b + 1)
                    for c in range(HA):
                        last = nc.scalar.activation(far[:, b, c, :], m["iotab"][:, :], ACT.Square, scale=-1.0,
                                                    bias=kg[:, bass.ds((i * 2 + b) * HG + c, 1)])
                    last.then_inc(squared, 1)
                    act.wait_ge(squared, i * 2 + b + 1)
                    nc.scalar.activation(hotp[:, b, 0:HA, :], far[:, b, :, :], ACT.Relu, bias=1.0, scale=-1.0).then_inc(hot_act, 1)

        @block.sync
        def _(sp):
            for work, sem in zip(sync_work, moved):
                work(sp, sem)

        @block.vector
        def _(dve):
            v = nc.vector
            link = linker(dve, dv, Steps())
            v.memset(zb[:, :], 0.0).then_inc(zs, 1)
            link(v.tensor_scalar(kf[:, :], key[:, :], 1.0 / NB, 0.5 / NB - 0.5, ALU.mult, ALU.add))
            v.tensor_scalar(kg[:, :], kf[:, :], MAGIC, -MAGIC, ALU.add, ALU.add).then_inc(keyed, 1)
            dve.wait_ge(keyed, 1)
            link(v.tensor_copy(keyp[:, :], kg[:, :]))
            link(v.scalar_tensor_tensor(keyj[:, :], kg[:, :], -float(NB), key[:, :], ALU.mult, ALU.add))
            with dve.Fori(0, HGROUNDS) as i:
                for b in range(2):
                    dve.wait_ge(used, i * 2 + b + 1)
                    at, atp = bass.ds((i * 2 + b) * HG, HG), bass.ds((i * 2 + b) * HG + HA, HG - HA)
                    v.tensor_tensor(hotp[:, b, HA:HG, :], m["iotab"][:, None, :].to_broadcast([P, HG - HA, P]),
                                    keyp[:, atp][:, :, None].to_broadcast([P, HG - HA, P]), ALU.is_equal).then_inc(hot, 1)
                    v.tensor_tensor(hotj[:, b, :, :], m["iotab"][:, None, 0:NB].to_broadcast([P, HG, NB]),
                                    keyj[:, at][:, :, None].to_broadcast([P, HG, NB]), ALU.is_equal).then_inc(hot, 1)
            dve.wait_ge(done, 1)
            link(v.tensor_copy(result[:, :], acc[:, 0:NB]))

        @block.tensor
        def _(pe):
            pe.wait_ge(zs, 1)
            nc.tensor.matmul(acc[:, 0:NB], zb[:, :], zb[:, 0:NB], start=True, stop=False).then_inc(used, 2)
            with pe.Fori(0, HGROUNDS) as i:
                for b in range(2):
                    pe.wait_ge(hot, i * 4 + b * 2 + 2)
                    pe.wait_ge(hot_act, i * 2 + b + 1)
                    for c in range(HG):
                        last = nc.tensor.matmul(acc[:, 0:NB], hotp[:, b, c, :], hotj[:, b, c, :], start=False, stop=False)
                    last.then_inc(used, 1)
            nc.tensor.matmul(acc[:, 0:NB], zb[:, :], zb[:, 0:NB], start=False, stop=True).then_inc(done, 1)


def zero_scratch(m):
    def work(sp, zeroed):
        ex = m["EX"][0:EP, :].rearrange("(p t) f -> p (t f)", p=P)
        for k in range(D):
            sp.dma_start(ex[:, k * T:(k + 1) * T], m["zero"][:, 0:T]).then_inc(zeroed, 16)
        sp.dma_start(m["EXD"][0:EP, :].rearrange("(p t) f -> p (t f)", p=P), m["zero"][:, 0:T]).then_inc(zeroed, 16)
        for table, width in ((m["SC"], D), (m["SC34"], D + 2)):
            sp.dma_start(table[EP:EP + 1, :], m["zero"][0:1, 0:width]).then_inc(zeroed, 16)
            sp.dma_start(table[EP + 1:EP + 1 + P, :], m["zero"][:, 0:width]).then_inc(zeroed, 16)
        sp.wait_ge(zeroed, 16 * (D + 5))
    return work


def copy_attributes(m, a, ordered):
    def work(sp, copied):
        sp.dma_start(m["efT"], a["efT"], cond=ordered).then_inc(copied, 16)
        sp.dma_start(m["sh"].rearrange("(p t) f -> p (t f)", p=P), a["sh"].rearrange("(p t) f -> p (t f)", p=P),
                     cond=ordered).then_inc(copied, 16)
        sp.wait_ge(copied, 32)
    return work


def degrees(nc, m):
    with Phase(nc, "de") as ph:
        dv = ph.sem("dv")
        block = ph.ctx.enter_context(nc.Block())

        @block.vector
        def _(dve):
            v = nc.vector
            link = linker(dve, dv, Steps())
            link(v.tensor_scalar(m["dinv"][:, :], m["deg"][:, :], 1.0, None, ALU.max))
            link(v.reciprocal(m["dinv"][:, :], m["dinv"][:, :]))
            link(v.memset(m["last"][:, :], 0.0))


def node_indices(nc, m, name):
    with Phase(nc, name) as ph:
        w = {k: ph.sb(k, [P, NB]) for k in ("scan", "end", "has", "t1", "t2")}
        zer = ph.sb("zer", [P, NB])
        tot = ph.sb("tot", [P, 1])
        off = ph.sb("off", [P, 1])
        tr = ph.sb("tr", [P, 1])
        offp = ph.ps("offp", [P, 512])
        dv, totals, offs = (ph.sem(n) for n in ("dv", "totals", "offs"))
        block = ph.ctx.enter_context(nc.Block())

        @block.vector
        def _(dve):
            v = nc.vector
            n = Steps()
            link = linker(dve, dv, n)
            link(v.tensor_scalar(m["cinv"][:, :], m["cnt"][:, :], 1.0, None, ALU.max))
            link(v.reciprocal(m["cinv"][:, :], m["cinv"][:, :]))
            link(v.memset(zer[:, :], 0.0))
            link(v.tensor_tensor_scan(w["scan"][:, :], m["cnt"][:, :], zer[:, :], 0.0, ALU.add, ALU.add))
            v.tensor_copy(tot[:, :], w["scan"][:, NB - 1:NB]).then_inc(totals, 1)
            dve.wait_ge(offs, 1)
            link(v.tensor_copy(off[:, :], offp[:, 0:1]))
            link(v.tensor_scalar(w["end"][:, :], w["scan"][:, :], off[:, 0:1], -1.0, ALU.add, ALU.add))
            link(v.tensor_tensor(w["t1"][:, :], w["end"][:, :], m["cnt"][:, :], ALU.subtract))
            link(v.tensor_scalar(w["t1"][:, :], w["t1"][:, :], 1.0, None, ALU.add))
            link(v.tensor_scalar(w["has"][:, :], m["cnt"][:, :], 0.5, None, ALU.is_gt))
            link(v.tensor_scalar(tr[:, :], m["rowid"][:, :], float(EP), None, ALU.add))
            link(v.tensor_scalar(w["t2"][:, :], w["t1"][:, :], tr[:, 0:1], None, ALU.subtract))
            link(v.tensor_tensor(w["t2"][:, :], w["t2"][:, :], w["has"][:, :], ALU.mult))
            link(v.tensor_scalar(w["t2"][:, :], w["t2"][:, :], tr[:, 0:1], None, ALU.add))
            link(v.tensor_copy(m["ixStart"][:, :], w["t2"][:, :]))
            link(v.tensor_scalar(w["t2"][:, :], w["end"][:, :], -float(EP), None, ALU.add))
            link(v.tensor_tensor(w["t2"][:, :], w["t2"][:, :], w["has"][:, :], ALU.mult))
            link(v.tensor_scalar(w["t2"][:, :], w["t2"][:, :], float(EP), None, ALU.add))
            link(v.tensor_copy(m["ixEnd"][:, :], w["t2"][:, :]))

        @block.tensor
        def _(pe):
            pe.wait_ge(totals, 1)
            nc.tensor.matmul(offp[:, 0:1], m["above"][:, :], tot[:, :], start=True, stop=True).then_inc(offs, 1)


def norm_relu(nc, m, name, x, out, table, scale=None):
    with Phase(nc, name) as ph:
        mean, var, dev = ph.sb("mean", [P, NB]), ph.sb("var", [P, NB]), ph.sb("dev", [P, NB])
        sq = ph.sb("sq", [P, NB, D])
        dv, va, sd, rows, stored = (ph.sem(n) for n in ("dv", "va", "sd", "rows", "stored"))
        block = ph.ctx.enter_context(nc.Block())
        wide = [P, NB, D]

        @block.vector
        def _(dve):
            v = nc.vector
            link = linker(dve, dv, Steps())
            link(v.tensor_reduce(mean[:, :], x[:, :, :], AX, ALU.add))
            link(v.tensor_scalar(mean[:, :], mean[:, :], 1.0 / D, None, ALU.mult))
            link(v.tensor_tensor(out[:, :, :], x[:, :, :], mean[:, :, None].to_broadcast(wide), ALU.subtract))
            link(v.tensor_tensor(sq[:, :, :], out[:, :, :], out[:, :, :], ALU.mult))
            link(v.tensor_reduce(var[:, :], sq[:, :, :], AX, ALU.add))
            v.tensor_scalar(var[:, :], var[:, :], 1.0 / D, EPS, ALU.mult, ALU.add).then_inc(va, 1)
            dve.wait_ge(sd, 1)
            link(v.reciprocal(dev[:, :], dev[:, :]))
            link(v.tensor_tensor(out[:, :, :], out[:, :, :], dev[:, :, None].to_broadcast(wide), ALU.mult))
            link(v.tensor_scalar(out[:, :, :], out[:, :, :], 0.0, None, ALU.max))
            if scale is None:
                v.tensor_copy(sq[:, :, :], out[:, :, :]).then_inc(rows, 1)
            else:
                v.tensor_tensor(sq[:, :, :], out[:, :, :], scale[:, :, None].to_broadcast(wide), ALU.mult).then_inc(rows, 1)

        @block.scalar
        def _(act):
            act.wait_ge(va, 1)
            nc.scalar.activation(dev[:, :], var[:, :], ACT.Sqrt).then_inc(sd, 1)

        @block.sync
        def _(sp):
            if table is not None:
                sp.wait_ge(rows, 1)
                sp.dma_start(table.rearrange("(p j) f -> p j f", p=P), sq[:, :, :]).then_inc(stored, 16)
                sp.wait_ge(stored, 16)


def store_rows(nc, name, table, rows, width):
    with Phase(nc, name) as ph:
        stored = ph.sem("stored")
        block = ph.ctx.enter_context(nc.Block())

        @block.sync
        def _(sp):
            sp.dma_start(table.rearrange("(p j) f -> p j f", p=P), rows[:, :, 0:width]).then_inc(stored, 16)
            sp.wait_ge(stored, 16)


class Starts:

    def __init__(self, m, ph, spread, rows, table, first):
        self.m, self.spread, self.rows, self.table, self.first = m, spread, rows, table, first
        self.put, self.got = ph.sem("put"), ph.sem("got")

    def fetch_first(self, pool):
        pool.indirect_dma_start(out=self.first[:, :], out_offset=None, in_=self.table,
                                in_offset=bass.IndirectOffsetOnAxis(ap=self.m["dst0"][:, 0:1], axis=0)).then_inc(self.got, 16)

    def scatter(self, pool, j):
        if j > 0:
            pool.wait_ge(self.put, 16 * j)
        ix = bass.IndirectOffsetOnAxis(ap=self.m["ixStart"][:, j:j + 1], axis=0)
        pool.indirect_dma_start(out=self.spread, out_offset=ix, in_=self.rows(j), in_offset=None).then_inc(self.put, 16)

    def finish(self, pool):
        pool.wait_ge(self.put, 16 * NB)
        pool.wait_ge(self.got, 16)


def scatter_to_starts(nc, m, name, *what):
    with Phase(nc, name) as ph:
        starts = Starts(m, ph, *what)
        block = ph.ctx.enter_context(nc.Block())

        @block.gpsimd
        def _(pool):
            starts.fetch_first(pool)
            for j in range(NB):
                starts.scatter(pool, j)
            starts.finish(pool)


def load_indices(sp, ix, src, ixin, free, first=0, rounds=ROUNDS):
    srcv = src.rearrange("(p t) -> p t", p=P)
    with sp.Fori(0, rounds) as i:
        for b in range(2):
            sp.wait_ge(free, i * 2 + b + 1)
            sp.dma_start(ix[:, b, :], srcv[:, bass.ds((i * 2 + b + first) * C, C)]).then_inc(ixin[b], 16)


def gather_rows(pool, ix, g, table, ixin, got, free, begun, rounds=ROUNDS, starts=None):
    def round_of_two(i, starts):
        for b in range(2):
            pool.wait_ge(free, i * 2 + b + 1)
            pool.wait_ge(ixin[b], i * 16 + 16)
            pool.sem_inc(begun, 1)
            for c in range(C):
                pool.indirect_dma_start(out=g[:, b, c, :], out_offset=None, in_=table,
                                        in_offset=bass.IndirectOffsetOnAxis(ap=ix[:, b, c:c + 1], axis=0)
                                        ).then_inc(got[b], 16)
                if starts and b * C + c < NB:
                    starts.scatter(pool, b * C + c)

    if starts:
        starts.fetch_first(pool)
        round_of_two(0, starts)
    with pool.Fori(1 if starts else 0, rounds) as i:
        round_of_two(i, None)
    if starts:
        starts.finish(pool)


class OneHotJob:

    def __init__(self, nc, m, ph, key, weights, result):
        self.nc, self.m, self.weights, self.result, self.key = nc, m, weights, result, key
        self.dt = F32 if weights else BF16
        self.iota = m["iota"] if weights else m["iotab"]
        self.keyp, self.keyj = ph.sb("keyp", [P, T], self.dt), ph.sb("keyj", [P, T], self.dt)
        self.kf = ph.sb("kf", [P, T])
        self.kg = self.keyp if weights else ph.sb("kg", [P, T])
        self.hotp = ph.sb("hotp", [P, 2, JG, P], self.dt)
        self.hotj = ph.sb("hotj", [P, 2, JG, NB], self.dt)
        self.hotw = ph.sb("hotw", [P, 2, JG, NB]) if weights else self.hotj
        self.zb = ph.sb("zb", [P, P], self.dt)
        self.acc = ph.ps("acc", [P, 512])
        self.hotp_made, self.hotj_made, self.used, self.zs, self.done = (
            ph.sem(k) for k in ("hotpmade", "hotjmade", "used", "zs2", "done"))

    def keys(self, link):
        v = self.nc.vector
        v.memset(self.zb[:, :], 0.0).then_inc(self.zs, 1)
        link(v.tensor_scalar(self.kf[:, :], self.key[:, :], 1.0 / NB, 0.5 / NB - 0.5, ALU.mult, ALU.add))
        link(v.tensor_scalar(self.kg[:, :], self.kf[:, :], MAGIC, -MAGIC, ALU.add, ALU.add))
        if not self.weights:
            link(v.tensor_copy(self.keyp[:, :], self.kg[:, :]))
        link(v.scalar_tensor_tensor(self.keyj[:, :], self.kg[:, :], -float(NB), self.key[:, :], ALU.mult, ALU.add))

    def one_hot_rows(self, dve, i, b):
        v = self.nc.vector
        for q in range(JN):
            g, k = b * JN + q, (b * JN + q) % 2
            at = bass.ds((i * 2 + b) * JC + q * JG, JG)
            dve.wait_ge(self.used, i * (2 * JN) + g + 1)
            v.tensor_tensor(self.hotj[:, k, :, :], self.iota[:, None, 0:NB].to_broadcast([P, JG, NB]),
                            self.keyj[:, at][:, :, None].to_broadcast([P, JG, NB]), ALU.is_equal).then_inc(self.hotj_made, 1)
            v.tensor_tensor(self.hotp[:, k, :, :], self.iota[:, None, :].to_broadcast([P, JG, P]),
                            self.keyp[:, at][:, :, None].to_broadcast([P, JG, P]), ALU.is_equal).then_inc(self.hotp_made, 1)
            if self.weights:
                dve.wait_ge(self.hotj_made, i * (4 * JN) + 2 * g + 1)
                v.tensor_tensor(self.hotw[:, k, :, :], self.hotj[:, k, :, :],
                                self.weights[:, at][:, :, None].to_broadcast([P, JG, NB]), ALU.mult).then_inc(self.hotj_made, 1)

    def products(self, pe):
        mm = self.nc.tensor.matmul
        pe.wait_ge(self.zs, 1)
        mm(self.acc[:, 0:NB], self.zb[:, :], self.zb[:, 0:NB], start=True, stop=False).then_inc(self.used, 2)
        per = 2 if self.weights else 1
        with pe.Fori(0, JROUNDS) as i:
            for g in range(2 * JN):
                k = g % 2
                pe.wait_ge(self.hotp_made, i * (2 * JN) + g + 1)
                pe.wait_ge(self.hotj_made, i * (2 * JN * per) + per * (g + 1))
                for c in range(JG):
                    last = mm(self.acc[:, 0:NB], self.hotp[:, k, c, :], self.hotw[:, k, c, :], start=False, stop=False)
                last.then_inc(self.used, 1)
        mm(self.acc[:, 0:NB], self.zb[:, :], self.zb[:, 0:NB], start=False, stop=True).then_inc(self.done, 1)

    def finish(self, dve, link):
        dve.wait_ge(self.done, 1)
        link(self.nc.vector.tensor_copy(self.result[:, :], self.acc[:, 0:NB]))


def gather_pass(nc, m, name, table, src, first=0, rounds=ROUNDS, job=None, starts=None):
    with Phase(nc, name) as ph:
        starts = Starts(m, ph, *starts) if starts else None
        job = OneHotJob(nc, m, ph, *job) if job else None
        ix = ph.sb("ix", [P, 2, C], I32)
        g = ph.sb("g", [P, 2, C, D])
        same = ph.sb("same", [P, D, S1])
        msg = ph.sb("msg", [P, D, S1])
        out = ph.sb("out", [P, D, S1])
        rows = ph.sb("rows", [P, C, D])
        free, begun, spread, scanned, packed, stored, zs, dv = (
            ph.sem(k) for k in ("free", "begun", "spread", "scanned", "packed", "stored", "zs", "dv"))
        ixin = [ph.sem(f"ixin{b}") for b in range(2)]
        got = [ph.sem(f"got{b}") for b in range(2)]
        block = ph.ctx.enter_context(nc.Block())
        scv = m["SC"][0:EP, :].rearrange("(p t) f -> p t f", p=P)

        @block.sync
        def _(sp):
            load_indices(sp, ix, src, ixin, free, first, rounds)

        @block.gpsimd
        def _(pool):
            gather_rows(pool, ix, g, table, ixin, got, free, begun, rounds, starts)

        @block.scalar
        def _(act):
            act.sem_inc(free, 2)
            act.wait_ge(zs, 2)
            with act.Fori(0, rounds) as i:
                for b in range(2):
                    nc.scalar.copy(same[:, :, 1:S1],
                                   m["same"][:, None, bass.ds((i * 2 + b + first) * C, C)].to_broadcast([P, D, C])).then_inc(spread, 1)
                    act.wait_ge(got[b], i * (16 * C) + 16 * C)
                    nc.scalar.copy(msg[:, :, 1:S1], g[:, b, :, :].rearrange("p c f -> p f c")).then_inc(free, 1)
                    act.wait_ge(scanned, i * 2 + b + 1)
                    nc.scalar.copy(rows[:, :, :], out[:, :, 1:S1].rearrange("p f c -> p c f")).then_inc(packed, 1)
                    act.wait_ge(packed, i * 2 + b + 1)
                    act.dma_start(scv[:, bass.ds((i * 2 + b + first) * C, C), :], rows[:, :, :]).then_inc(stored, 16)
                    act.wait_ge(stored, i * 32 + (b + 1) * 16)

        @block.vector
        def _(dve):
            v = nc.vector
            n = Steps()
            link = linker(dve, dv, n)
            v.memset(same[:, :, 0:1], 0.0).then_inc(zs, 1)
            v.tensor_copy(out[:, :, C:S1], m["last"][:, 0:D, None]).then_inc(zs, 1)
            dve.wait_ge(zs, 2)
            if job:
                job.keys(link)
            with dve.Fori(0, rounds) as i:
                n.enter(i, 2)
                for b in range(2):
                    link(v.tensor_copy(msg[:, :, 0:1], out[:, :, C:S1]))
                    if job:
                        job.one_hot_rows(dve, i, b)
                    dve.wait_ge(free, i * 2 + b + 3)
                    dve.wait_ge(spread, i * 2 + b + 1)
                    v.tensor_tensor_scan(out[:, :, :].rearrange("p f c -> p (f c)"), same[:, :, :].rearrange("p f c -> p (f c)"),
                                         msg[:, :, :].rearrange("p f c -> p (f c)"), 0.0, ALU.mult, ALU.add).then_inc(scanned, 1)
                    dve.wait_ge(packed, i * 2 + b + 1)
            n.leave(rounds)
            dve.wait_ge(scanned, 2 * rounds)
            link(v.tensor_copy(m["last"][:, 0:D], out[:, :, C]))
            if job:
                job.finish(dve, link)

        @block.tensor
        def _(pe):
            if job:
                job.products(pe)


def carry_and_collect(nc, m, name):
    with Phase(nc, name) as ph:
        pad = ph.sb("pad", [P, 2, P])
        padT = ph.sb("padT", [P, 2, P])
        carT = ph.sb("carT", [P, P + 1])
        row, patched = ph.sb("row", [P, D]), ph.sb("patched", [P, D])
        psT = ph.ps("psT", [P, 512])
        dv, ready, turned, scanned, back, added, read, put, got = (
            ph.sem(k) for k in ("dv", "ready", "turned", "scanned", "back", "added", "read", "put", "got"))
        block = ph.ctx.enter_context(nc.Block())

        @block.vector
        def _(dve):
            v = nc.vector
            link = linker(dve, dv, Steps())
            link(v.memset(pad[:, :, :], 0.0))
            link(v.memset(carT[:, :], 0.0))
            v.tensor_copy(pad[:, 0, 0:D], m["last"][:, 0:D]).then_inc(ready, 1)
            v.tensor_copy(pad[:, 1, 0:D], m["whole"][:, 0:1].to_broadcast([P, D])).then_inc(ready, 1)
            dve.wait_ge(turned, 2)
            link(v.tensor_copy(padT[:, :, :], psT[:, 0:2 * P].rearrange("p (k c) -> p k c", k=2)))
            v.tensor_tensor_scan(carT[:, 1:P + 1], padT[:, 1, :], padT[:, 0, :], 0.0, ALU.mult, ALU.add).then_inc(scanned, 1)
            dve.wait_ge(back, 1)
            dve.wait_ge(read, 16)
            v.tensor_tensor(patched[:, :], row[:, :], psT[:, 2 * P:2 * P + D], ALU.add).then_inc(added, 1)
            link(v.memset(m["last"][:, :], 0.0))

        @block.tensor
        def _(pe):
            pe.wait_ge(ready, 2)
            nc.tensor.transpose(psT[:, 0:P], pad[:, 0, :], m["ident"][:, :]).then_inc(turned, 1)
            nc.tensor.transpose(psT[:, P:2 * P], pad[:, 1, :], m["ident"][:, :]).then_inc(turned, 1)
            pe.wait_ge(scanned, 1)
            nc.tensor.transpose(psT[:, 2 * P:3 * P], carT[:, 0:P], m["ident"][:, :]).then_inc(back, 1)

        @block.gpsimd
        def _(pool):
            to = bass.IndirectOffsetOnAxis(ap=m["ixPatch"][:, 0:1], axis=0)
            pool.indirect_dma_start(out=row[:, :], out_offset=None, in_=m["SC"], in_offset=to).then_inc(read, 16)
            pool.wait_ge(added, 1)
            pool.indirect_dma_start(out=m["SC"], out_offset=to, in_=patched[:, :], in_offset=None).then_inc(put, 16)
            pool.wait_ge(put, 16)
            for j in range(NB):
                pool.indirect_dma_start(out=m["agg"][:, j, :], out_offset=None, in_=m["SC"],
                                        in_offset=bass.IndirectOffsetOnAxis(ap=m["ixEnd"][:, j:j + 1], axis=0)).then_inc(got, 16)
            pool.wait_ge(got, 16 * NB)


def expand_degrees(nc, m):
    with Phase(nc, "xd") as ph:
        ex = ph.sb("ex", [P, T])
        dv, loaded = ph.sem("dv"), ph.sem("loaded")
        block = ph.ctx.enter_context(nc.Block())

        @block.sync
        def _(sp):
            sp.dma_start(ex[:, :], m["EXD"][0:EP, :].rearrange("(p t) f -> p (t f)", p=P)).then_inc(loaded, 16)
            sp.wait_ge(loaded, 16)

        @block.vector
        def _(dve):
            link = linker(dve, dv, Steps())
            dve.wait_ge(loaded, 16)
            link(nc.vector.tensor_tensor_scan(m["wts"][:, :], m["same"][:, :], ex[:, :], m["firstd"][:, 0:1], ALU.mult, ALU.add))


def hamilton_gradient(nc, m, a):
    with Phase(nc, "hg") as ph:
        w1b = ph.sb("w1b", [P, 4, P])
        w1 = ph.sb("w1", [D, P])
        jt = ph.sb("jt", [D, D])
        w2 = ph.sb("w2", [P, D])
        w2s = ph.sb("w2s", [P, 1])
        b1 = ph.sb("b1", [P, 1])
        rw = ph.sb("rw", [P, D])
        coef = ph.sb("coef", [P, NB])
        slot, slotT = ph.sb("slot", [P, 4 * D]), ph.sb("slotT", [P, P])
        th, sq, gr = (ph.sb(k, [P, 4 * P]) for k in ("th", "sq", "gr"))
        psT, psZ, psU, psW = (ph.ps(k, [P, 512]) for k in ("psT", "psZ", "psU", "psW"))
        names = ("dv", "zeroed", "loaded", "jw", "weights", "slotted", "turned", "flat", "hidden", "tanhed", "grads", "back")
        dv, zeroed, loaded, jw, weights, slotted, turned, flat, hidden, tanhed, grads, back = (ph.sem(k) for k in names)
        block = ph.ctx.enter_context(nc.Block())

        @block.sync
        def _(sp):
            sp.wait_ge(zeroed, 1)
            for b in range(4):
                sp.dma_start(w1b[D * b:D * b + D, b, :], a["W1"]).then_inc(loaded, 16)
            for dst, src in ((w1, "W1"), (jt, "JT"), (w2, "W2"), (b1, "b1")):
                sp.dma_start(dst[:, :], a[src]).then_inc(loaded, 16)
            sp.wait_ge(loaded, 128)

        @block.vector
        def _(dve):
            v = nc.vector
            n = Steps()
            link = linker(dve, dv, n)
            v.memset(w1b[:, :, :], 0.0).then_inc(zeroed, 1)
            link(v.tensor_tensor(coef[:, :], m["dinv"][:, :], m["tsum"][:, :], ALU.mult))
            dve.wait_ge(loaded, 128)
            link(v.tensor_reduce(w2s[:, :], w2[:, :], AX, ALU.add))
            dve.wait_ge(jw, 1)
            v.tensor_scalar(rw[:, :], psW[:, 0:D], w2s[:, 0:1], None, ALU.mult).then_inc(weights, 1)
            with dve.Fori(0, NG) as g:
                n.enter(g, 2)
                dve.wait_ge(tanhed, g + 1)
                link(v.tensor_tensor(sq[:, :], th[:, :], th[:, :], ALU.mult))
                v.tensor_scalar(gr[:, :], sq[:, :], -1.0, 1.0, ALU.mult, ALU.add).then_inc(grads, 1)
                dve.wait_ge(back, g + 1)
                link(v.tensor_tensor(m["H"][:, bass.ds(g * 4, 4), :], psU[:, 0:4 * D].rearrange("p (b f) -> p b f", b=4),
                                     coef[:, bass.ds(g * 4, 4)][:, :, None].to_broadcast([P, 4, D]), ALU.mult))
            n.leave(NG)

        @block.scalar
        def _(act):
            act.wait_ge(loaded, 128)
            with act.Fori(0, NG) as g:
                nc.scalar.copy(slot[:, :].rearrange("p (b f) -> p b f", b=4), m["agg"][:, bass.ds(g * 4, 4), :]).then_inc(slotted, 1)
                act.wait_ge(turned, g + 1)
                nc.scalar.copy(slotT[:, :], psT[:, 0:P]).then_inc(flat, 1)
                act.wait_ge(hidden, g + 1)
                nc.scalar.activation(th[:, :], psZ[:, :], ACT.Tanh, bias=b1[:, 0:1]).then_inc(tanhed, 1)

        @block.tensor
        def _(pe):
            pe.wait_ge(loaded, 128)
            nc.tensor.matmul(psW[:, 0:D], w1[:, :], jt[:, :], start=True, stop=True).then_inc(jw, 1)
            pe.wait_ge(weights, 1)
            with pe.Fori(0, NG) as g:
                pe.wait_ge(slotted, g + 1)
                nc.tensor.transpose(psT[:, 0:P], slot[:, :], m["ident"][:, :]).then_inc(turned, 1)
                pe.wait_ge(flat, g + 1)
                for b in range(4):
                    last = nc.tensor.matmul(psZ[:, b * P:(b + 1) * P], w1b[:, b, :], slotT[:, :], start=True, stop=True)
                last.then_inc(hidden, 1)
                pe.wait_ge(grads, g + 1)
                for b in range(4):
                    last = nc.tensor.matmul(psU[:, b * D:(b + 1) * D], gr[:, b * P:(b + 1) * P], rw[:, :], start=True, stop=True)
                last.then_inc(back, 1)


def scatter_pass(nc, m):
    Q, B4 = 4, C // 4
    AHEAD = 5
    with Phase(nc, "sc") as ph:
        ex = ph.sb("ex", [P, 2, C, D])
        same = ph.sb("same", [P, D, S1])
        msg = ph.sb("msg", [P, D, S1])
        val = ph.sb("val", [P, 2, D, S1])
        sid = ph.sb("sid", [P, 2, C])
        tos = ph.sb("tos", [P, 2, C])
        eq = ph.sb("eq", [P, 2, Q, P])
        earlier = ph.sb("earlier", [P, Q, P])
        dup = ph.sb("dup", [P, 3, Q])
        trash = ph.sb("trash", [P, 1])
        vals = ph.sb("vals", [P, 2, Q, D])
        ids = ph.sb("ids", [P, 2, Q], I32)
        psB = [ph.ps(f"psB{k}", [P, 512]) for k in range(2)]
        psV = [ph.ps(f"psV{k}", [P, 512]) for k in range(2)]
        names = ("dv", "zs", "taken", "spread", "msgs", "scanned", "named", "wide", "equal", "summed", "copied", "aimed", "go")
        dv, zs, taken, spread, msgs, scanned, named, wide, equal, summed, copied, aimed, go = (ph.sem(k) for k in names)
        exin = [ph.sem(f"exin{b}") for b in range(2)]
        chain = [ph.sem(f"chain{k}") for k in range(CHAINS)]
        block = ph.ctx.enter_context(nc.Block())
        exv = m["EX"][0:EP, :].rearrange("(p t) f -> p t f", p=P)

        @block.sync
        def _(sp):
            with sp.Fori(0, ROUNDS) as i:
                for b in range(2):
                    sp.wait_ge(taken, i * 2 + b + 1)
                    sp.dma_start(ex[:, b, :, :], exv[:, bass.ds((i * 2 + b) * C, C), :]).then_inc(exin[b], 16)

        @block.scalar
        def _(act):
            act.sem_inc(taken, 2)
            act.sem_inc(copied, 2)
            act.wait_ge(zs, 2)

            def prepare(i, b):
                nc.scalar.copy(same[:, :, 1:S1],
                               m["same"][:, None, bass.ds((i * 2 + b) * C, C)].to_broadcast([P, D, C])).then_inc(spread, 1)
                act.wait_ge(exin[b % 2], i * 16 + 16 * (b // 2 + 1))
                nc.scalar.copy(msg[:, :, 1:S1], ex[:, b % 2, :, :].rearrange("p c f -> p f c")).then_inc(taken, 1)

            def round_of_two(i, chunks):
                for b in range(2):
                    for q in range(B4):
                        lb = b * B4 + q
                        k = lb % 2
                        act.wait_ge(summed, i * (2 * B4) + lb + 3)
                        for r in range(Q):
                            act.wait_ge(chain[k * Q + r], i * (16 * B4) + 16 * (lb // 2 + 1))
                        nc.scalar.copy(vals[:, k, :, :], psV[k][:, 0:Q * D].rearrange("p (r f) -> p r f", r=Q)).then_inc(copied, 1)
                        if q == AHEAD and b < chunks:
                            prepare(i, b + 1)

            prepare(0, 0)
            with act.Fori(0, ROUNDS - 1) as i:
                round_of_two(i, 2)
            round_of_two(ROUNDS - 1, 1)

        @block.vector
        def _(dve):
            v = nc.vector
            n = Steps()
            link = linker(dve, dv, n)
            v.memset(same[:, :, 0:1], 0.0).then_inc(zs, 1)
            v.tensor_copy(val[:, 1, :, C:S1], m["first"][:, :, None]).then_inc(zs, 1)
            dve.wait_ge(zs, 2)
            link(v.tensor_scalar(trash[:, :], m["rowid"][:, :], float(NP), None, ALU.add))

            def prepare(i, b):
                w, j = b % 2, i * 2 + b
                v.tensor_copy(sid[:, w, :], m["srcf"][:, bass.ds(j * C, C)]).then_inc(named, 1)
                v.tensor_scalar(tos[:, w, :], m["srcf"][:, bass.ds(j * C, C)], -1.0, trash[:, 0:1],
                                ALU.mult, ALU.add).then_inc(named, 1)
                link(v.tensor_copy(msg[:, :, 0:1], val[:, 1 - w, :, C:S1]))
                dve.wait_ge(spread, i * 2 + b + 1)
                dve.wait_ge(taken, i * 2 + b + 3)
                v.tensor_tensor_scan(val[:, w, :, :].rearrange("p f c -> p (f c)"), same[:, :, :].rearrange("p f c -> p (f c)"),
                                     msg[:, :, :].rearrange("p f c -> p (f c)"), 0.0, ALU.mult, ALU.add).then_inc(scanned, 1)
                dve.wait_ge(scanned, i * 2 + b + 1)
                dve.wait_ge(named, i * 4 + b * 2 + 2)

            def round_of_two(i, chunks):
                for b in range(2):
                    for q in range(B4):
                        lb = b * B4 + q
                        k = lb % 2
                        c = q * Q
                        dve.wait_ge(wide, i * (2 * B4) + lb + 1)
                        dve.wait_ge(summed, i * (2 * B4) + lb + 1)
                        v.tensor_tensor(eq[:, k, :, :], psB[k][:, :].rearrange("p (r c) -> p r c", r=Q),
                                        sid[:, b, c:c + Q][:, :, None].to_broadcast([P, Q, P]), ALU.is_equal).then_inc(equal, 1)
                        dve.wait_ge(equal, i * (2 * B4) + lb + 1)
                        link(v.tensor_tensor(earlier[:, :, :], eq[:, k, :, :],
                                             m["below"][:, None, :].to_broadcast([P, Q, P]), ALU.mult))
                        link(v.tensor_reduce(dup[:, 0, :], earlier[:, :, :], AX, ALU.add))
                        link(v.tensor_scalar(dup[:, 1, :], dup[:, 0, :], 0.5, None, ALU.is_gt))
                        link(v.tensor_tensor(dup[:, 2, :], dup[:, 1, :], tos[:, b, c:c + Q], ALU.mult))
                        for r in range(Q):
                            dve.wait_ge(chain[k * Q + r], i * (16 * B4) + 16 * (lb // 2 + 1))
                        v.tensor_tensor(ids[:, k, :], dup[:, 2, :], sid[:, b, c:c + Q], ALU.add).then_inc(aimed, 1)
                        if q == AHEAD and b < chunks:
                            prepare(i, b + 1)

            prepare(0, 0)
            with dve.Fori(0, ROUNDS - 1) as i:
                n.enter(i, 2 * (1 + B4 * 4))
                round_of_two(i, 2)
            n.leave(ROUNDS - 1)
            round_of_two(ROUNDS - 1, 1)

        @block.tensor
        def _(pe):
            pe.sem_inc(summed, 2)
            with pe.Fori(0, ROUNDS) as i:
                for b in range(2):
                    pe.wait_ge(named, i * 4 + b * 2 + 1)
                    for q in range(B4):
                        lb = b * B4 + q
                        k = lb % 2
                        c = q * Q
                        for r in range(Q):
                            last = nc.tensor.matmul(psB[k][:, r * P:(r + 1) * P], sid[:, b, c + r:c + r + 1].to_broadcast([P, P]),
                                                    m["ident"][:, :], start=True, stop=True)
                        last.then_inc(wide, 1)
                        pe.wait_ge(equal, i * (2 * B4) + lb + 1)
                        pe.wait_ge(copied, i * (2 * B4) + lb + 1)
                        for r in range(Q):
                            last = nc.tensor.matmul(psV[k][:, r * D:(r + 1) * D], eq[:, k, r, :], val[:, b, :, 1 + c + r],
                                                    start=True, stop=True)
                        last.then_inc(summed, 1)

        @block.gpsimd
        def _(pool):
            for k in range(CHAINS):
                pool.dma_start(m[f"ACC{k}"].rearrange("(p j) f -> p (j f)", p=P), m["zero"][:, :]).then_inc(chain[k], 16)
            with pool.Fori(0, ROUNDS) as i:
                for lb in range(2 * B4):
                    k = lb % 2
                    pool.wait_ge(copied, i * (2 * B4) + lb + 3)
                    pool.wait_ge(aimed, i * (2 * B4) + lb + 1)
                    pool.sem_inc(go, 1)
                    for r in range(Q):
                        pool.indirect_dma_start(out=m[f"ACC{k * Q + r}"], in_=vals[:, k, r, :], in_offset=None,
                                                out_offset=bass.IndirectOffsetOnAxis(ap=ids[:, k, r:r + 1], axis=0),
                                                compute_op=ALU.add).then_inc(chain[k * Q + r], 16)
            for k in range(CHAINS):
                pool.wait_ge(chain[k], 16 * (1 + T // CHAINS))


def add_gradient(nc, m):
    with Phase(nc, "ag") as ph:
        part = ph.sb("part", [P, 2, NB, D])
        dv, added = ph.sem("dv"), ph.sem("added")
        got = [ph.sem(f"got{b}") for b in range(2)]
        block = ph.ctx.enter_context(nc.Block())

        @block.sync
        def _(sp):
            for k in range(CHAINS):
                if k >= 2:
                    sp.wait_ge(added, k - 1)
                sp.dma_start(part[:, k % 2, :, :], m[f"ACC{k}"][0:NP, :].rearrange("(p j) f -> p j f", p=P)).then_inc(got[k % 2], 16)

        @block.vector
        def _(dve):
            link = linker(dve, dv, Steps())
            for k in range(CHAINS):
                dve.wait_ge(got[k % 2], 16 * (k // 2 + 1))
                if k == 0:
                    nc.vector.tensor_copy(m["agg"][:, :, :], part[:, 0, :, :]).then_inc(added, 1)
                else:
                    nc.vector.tensor_tensor(m["agg"][:, :, :], m["agg"][:, :, :], part[:, k % 2, :, :], ALU.add).then_inc(added, 1)
                dve.wait_ge(added, k + 1)
            link(nc.vector.tensor_tensor(m["agg"][:, :, :], m["agg"][:, :, :], m["dinv"][:, :, None].to_broadcast([P, NB, D]), ALU.mult))
            link(nc.vector.tensor_tensor(m["X"][:, :, :], m["X"][:, :, :], m["agg"][:, :, :], ALU.add))


def product_pass(nc, m, a):
    Q, B4 = 4, C // 4
    with Phase(nc, "pp") as ph:
        ix = ph.sb("ix", [P, 2, C], I32)
        g = ph.sb("g", [P, 2, C, D])
        ef = ph.sb("ef", [P, 2, B4 * P])
        sh = ph.sb("sh", [P, 2, C, 4])
        v1 = ph.sb("v1", [P, 2, P])
        c1 = ph.sb("c1", [P, 1])
        v2 = ph.sb("v2", [P, 2, WN])
        b2 = ph.sb("b2", [1, 3, WN])
        b2p = ph.sb("b2p", [P, 2, WN], BF16)
        b2r = ph.sb("b2r", [1, 3, 2, WN], BF16)
        ones = ph.sb("ones", [P, P], BF16)
        hid = ph.sb("hid", [P, 2, 2 * P])
        ab = ph.sb("ab", [P, C, 16])
        vs = ph.sb("vs", [P, C, MUL, 3])
        vp = ph.sb("vp", [P, C, MUL * 3])
        p1 = ph.sb("p1", [P, 2, Q, 128])
        p2 = ph.sb("p2", [P, 2, 4, Q, 64])
        pq = ph.sb("pq", [P, 4, C, MUL])
        pm = ph.sb("pm", [P, 3, C, MUL])
        same = ph.sb("same", [P, D, S1])
        msg = ph.sb("msg", [P, D, S1])
        out = ph.sb("out", [P, 2, D, S1])
        rows = ph.sb("rows", [P, C, D])
        psH = [ph.ps(f"psH{k}", [P, 512]) for k in range(2)]
        psW = [ph.ps(f"psW{k}", [P, Q, WN]) for k in range(2)]
        names = ("free", "begun", "spread", "scanned", "packed", "stored", "zs", "dv", "weights", "ready", "hidden", "relued", "wide", "used", "summed", "split", "biased")
        free, begun, spread, scanned, packed, stored, zs, dv, weights, ready, hidden, relued, wide, used, summed, split, biased = (ph.sem(k) for k in names)
        ixin = [ph.sem(f"ixin{b}") for b in range(2)]
        got = [ph.sem(f"got{b}") for b in range(2)]
        efin = [ph.sem(f"efin{b}") for b in range(2)]
        block = ph.ctx.enter_context(nc.Block())
        scv = m["SC"][0:EP, :].rearrange("(p t) f -> p t f", p=P)
        shv = m["sh"].rearrange("(p t) f -> p t f", p=P)
        srcv = m["src"].rearrange("(p t) -> p t", p=P)
        NBAT = 2 * B4

        @block.sync
        def _(sp):
            sp.wait_ge(zs, 6)
            for r in range(4):
                sp.dma_start(v1[D * r:D * r + D, r // 2, HID1 * (r % 2):HID1 * (r % 2) + HID1], a["V1"]).then_inc(weights, 16)
            for r in range(2):
                sp.dma_start(c1[HID1 * r:HID1 * r + HID1, :], a["c1"]).then_inc(weights, 16)
                sp.dma_start(v2[HID1 * r:HID1 * r + HID1, r, :], a["V2"][0:HID1, :]).then_inc(weights, 16)
            sp.dma_start(b2[:, 0, :], a["V2"][HID1:HID1 + 1, :]).then_inc(weights, 16)
            sp.wait_ge(split, 1)
            for r in range(3):
                sp.dma_start(b2p[r:r + 1, :, :], b2r[:, r, :, :]).then_inc(biased, 16)
            with sp.Fori(0, ROUNDS) as i:
                for b in range(2):
                    at = bass.ds((i * 2 + b) * C, C)
                    sp.wait_ge(free, i * 2 + b + 1)
                    sp.dma_start(ix[:, b, :], srcv[:, at]).then_inc(ixin[b], 16)
                    sp.dma_start(sh[:, b, :, :], shv[:, at, :]).then_inc(efin[b], 16)
                    sp.dma_start(ef[:, b, :], m["efT"][:, bass.ds((i * 2 + b) * (B4 * P), B4 * P)]).then_inc(efin[b], 16)

        @block.gpsimd
        def _(pool):
            gather_rows(pool, ix, g, m["HT"], ixin, got, free, begun)

        @block.scalar
        def _(act):
            act.wait_ge(weights, 144)
            act.wait_ge(zs, 6)
            act.dma_start(scv[:, 0:1, :], rows[:, 0:1, :]).then_inc(stored, 16)
            with act.Fori(0, ROUNDS) as i:
                for b in range(2):
                    nc.scalar.copy(same[:, :, 1:S1],
                                   m["same"][:, None, bass.ds((i * 2 + b) * C, C)].to_broadcast([P, D, C])).then_inc(spread, 1)
                    for q in range(B4):
                        lb = b * B4 + q
                        k = lb % 2
                        act.wait_ge(hidden, i * NBAT + lb + 1)
                        act.wait_ge(wide, i * NBAT + lb + 1)
                        nc.scalar.activation(hid[:, k, :], psH[k][:, 0:2 * P], ACT.Relu, bias=c1[:, 0:1]).then_inc(relued, 1)
                    act.wait_ge(scanned, i * 2 + b + 1)
                    act.wait_ge(stored, i * 32 + b * 16 + 16)
                    nc.scalar.copy(rows[:, :, :], out[:, b, :, 1:S1].rearrange("p f c -> p c f")).then_inc(packed, 1)
                    act.wait_ge(packed, i * 2 + b + 2)
                    act.dma_start(scv[:, bass.ds((i * 2 + b) * C, C), :], rows[:, :, :]).then_inc(stored, 16)

        @block.tensor
        def _(pe):
            pe.sem_inc(wide, 2)
            pe.wait_ge(ready, 1)
            pe.wait_ge(biased, 48)
            with pe.Fori(0, ROUNDS) as i:
                for b in range(2):
                    pe.wait_ge(efin[b], i * 32 + 32)

                    def hidden_layer(q):
                        k = (b * B4 + q) % 2
                        for h in range(2):
                            last = nc.tensor.matmul(psH[k][:, h * P:(h + 1) * P], v1[:, h, :], ef[:, b, q * P:(q + 1) * P],
                                                    start=True, stop=True)
                        last.then_inc(hidden, 1)
                    hidden_layer(0)
                    for q in range(B4):
                        lb = b * B4 + q
                        k = lb % 2
                        if q + 1 < B4:
                            hidden_layer(q + 1)
                        pe.wait_ge(relued, i * NBAT + lb + 1)
                        pe.wait_ge(used, i * NBAT + lb + 1)
                        for h in range(2):
                            two = psW[k][:, 2 * h:2 * h + 2, :].rearrange("p r w -> p (r w)")
                            nc.tensor.matmul(two, hid[:, k, h * P:(h + 1) * P], v2[:, :, :].rearrange("p r w -> p (r w)"),
                                             start=True, stop=False)
                            last = nc.tensor.matmul(two, ones[:, :], b2p[:, :, :].rearrange("p r w -> p (r w)"),
                                                    start=False, stop=True)
                        last.then_inc(wide, 1)

        @block.vector
        def _(dve):
            v = nc.vector
            n = Steps()
            link = linker(dve, dv, n)
            dve.sem_inc(free, 2)
            dve.sem_inc(packed, 1)
            dve.sem_inc(used, 2)
            dve.sem_inc(summed, 4)
            v.memset(same[:, :, 0:1], 0.0).then_inc(zs, 1)
            v.memset(out[:, 1, :, C:S1], 0.0).then_inc(zs, 1)
            v.memset(rows[:, 0:1, :], 0.0).then_inc(zs, 1)
            v.memset(v1[:, :, :], 0.0).then_inc(zs, 1)
            v.memset(v2[:, :, :], 0.0).then_inc(zs, 1)
            v.memset(b2p[:, :, :], 0.0).then_inc(zs, 1)
            link(v.memset(ones[:, :], 1.0))
            dve.wait_ge(zs, 6)
            dve.wait_ge(weights, 144)
            for w in (v2[:, 0, :], v2[:, 1, :], b2[:, 0, :]):
                link(v.tensor_scalar(w, w, ALPHA, None, ALU.mult))
                pair = w[:, 0:128].rearrange("k (o h i) -> k o h i", o=MUL, h=2)[:, :, 1, :]
                link(v.tensor_scalar(pair, pair, C110, None, ALU.mult))
            for r in range(3):
                link(v.tensor_copy(b2r[:, r, 0, :], b2[:, r, :]))
                link(v.tensor_copy(b2r[:, r, 1, :], b2[:, r, :]))
                if r < 2:
                    link(v.tensor_tensor(b2[:, r + 1, :], b2[:, r, :], b2r[:, r, 0, :], ALU.subtract))
            dve.sem_inc(split, 1)
            dve.sem_inc(ready, 1)
            with dve.Fori(0, ROUNDS) as i:
                n.enter(i, 2 * 5)
                for b in range(2):
                    dve.wait_ge(got[b], i * (16 * C) + 16 * C)
                    dve.wait_ge(efin[b], i * 32 + 32)
                    s_, v_ = g[:, b, :, 0:MUL], g[:, b, :, MUL:D]
                    v.tensor_tensor(ab[:, :, 0:MUL], s_, sh[:, b, :, 0:1].to_broadcast([P, C, MUL]), ALU.mult)
                    v.tensor_tensor(vp[:, :, :], v_, sh[:, b, :, 0:1].to_broadcast([P, C, 3 * MUL]), ALU.mult)
                    link(v.tensor_tensor(vs[:, :, :, :], v_.rearrange("p c (i x) -> p c i x", x=3),
                                         sh[:, b, :, None, 1:4].to_broadcast([P, C, MUL, 3]), ALU.mult))
                    link(v.tensor_reduce(ab[:, :, MUL:16], vs[:, :, :, :], AX, ALU.add))

                    def sums(q):
                        k, c = (b * B4 + q) % 2, q * Q
                        dve.wait_ge(used, i * NBAT + b * B4 + q + 3)
                        v.tensor_reduce(msg[:, 0:MUL, 1 + c:1 + c + Q].rearrange("p o r -> p r o"),
                                        p1[:, k, :, :].rearrange("p r (o j) -> p r o j", o=MUL), AX, ALU.add).then_inc(summed, 1)
                        v.tensor_reduce(pq[:, :, c:c + Q, :],
                                        p2[:, k, :, :, :].rearrange("p x r (o j) -> p x (r o) j", o=MUL), AX, ALU.add).then_inc(summed, 1)

                    for q in range(B4):
                        lb = b * B4 + q
                        k = lb % 2
                        c = q * Q
                        shape = [P, Q, MUL, MUL]
                        dve.wait_ge(wide, i * NBAT + lb + 3)
                        dve.wait_ge(summed, i * (2 * NBAT) + lb * 2 + 2)
                        v.tensor_tensor(p1[:, k, :, :].rearrange("p r (o j) -> p r o j", o=MUL),
                                        psW[k][:, :, 0:128].rearrange("p r (o j) -> p r o j", o=MUL),
                                        ab[:, c:c + Q, None, :].to_broadcast([P, Q, MUL, 16]), ALU.mult)
                        v.tensor_tensor(p2[:, k, 0, :, :].rearrange("p r (o j) -> p r o j", o=MUL),
                                        psW[k][:, :, 128:192].rearrange("p r (o j) -> p r o j", o=MUL),
                                        s_[:, c:c + Q, None, :].to_broadcast(shape), ALU.mult)
                        for x in range(3):
                            last = v.tensor_tensor(p2[:, k, 1 + x, :, :].rearrange("p r (o j) -> p r o j", o=MUL),
                                                   psW[k][:, :, 192:256].rearrange("p r (o j) -> p r o j", o=MUL),
                                                   vp[:, c:c + Q, None, x::3].to_broadcast(shape), ALU.mult)
                        last.then_inc(used, 1)
                        if q >= 1:
                            sums(q - 1)
                    sums(B4 - 1)
                    dve.wait_ge(summed, i * (2 * NBAT) + (b + 1) * 2 * B4 + 4)
                    mv = msg[:, MUL:D, 1:S1].rearrange("p (o x) c -> p x c o", x=3)
                    for x in range(3):
                        last = v.tensor_tensor(pm[:, x, :, :], pq[:, 0, :, :],
                                               sh[:, b, :, 1 + x:2 + x].to_broadcast([P, C, MUL]), ALU.mult)
                    link(last)
                    link(v.tensor_tensor(mv, pm[:, :, :, :], pq[:, 1:4, :, :], ALU.add))
                    link(v.tensor_copy(msg[:, :, 0:1], out[:, 1 - b, :, C:S1]))
                    dve.wait_ge(spread, i * 2 + b + 1)
                    v.tensor_tensor_scan(out[:, b, :, :].rearrange("p f c -> p (f c)"), same[:, :, :].rearrange("p f c -> p (f c)"),
                                         msg[:, :, :].rearrange("p f c -> p (f c)"), 0.0, ALU.mult, ALU.add).then_inc(scanned, 1)
                    dve.wait_ge(scanned, i * 2 + b + 1)
                    dve.sem_inc(free, 1)
                    dve.wait_ge(packed, i * 2 + b + 1)
            n.leave(ROUNDS)
            link(v.tensor_copy(m["last"][:, 0:D], out[:, 1, :, C]))
            dve.wait_ge(stored, 16 * (CHUNKS + 1))


def dense(nc, m, name, terms, width, weight, finish, steps, extra=()):
    K = len(terms)
    with Phase(nc, name) as ph:
        wb = [ph.sb(f"wb{k}", [P, 4, width]) for k in range(K)]
        slot, slotT = ph.sb("slot", [P, K, 4 * D]), ph.sb("slotT", [P, K, P])
        psT, psO = ph.ps("psT", [P, 512]), ph.ps("psO", [P, 512])
        dv, zeroed, loaded, slotted, turned, flat, made = (
            ph.sem(k) for k in ("dv", "zeroed", "loaded", "slotted", "turned", "flat", "made"))
        count = [0]
        block = ph.ctx.enter_context(nc.Block())

        @block.sync
        def _(sp):
            sp.wait_ge(zeroed, K)
            for k in range(K):
                count[0] += weight(sp, k, wb[k], loaded)
            for dst, src in extra:
                sp.dma_start(dst, src).then_inc(loaded, 16)
                count[0] += 1
            sp.wait_ge(loaded, 16 * count[0])

        @block.scalar
        def _(act):
            with act.Fori(0, NG) as g:
                for k in range(K):
                    nc.scalar.copy(slot[:, k, :].rearrange("p (b f) -> p b f", b=4), terms[k][:, bass.ds(g * 4, 4), :]).then_inc(slotted, 1)
                act.wait_ge(turned, g + 1)
                nc.scalar.copy(slotT[:, :, :], psT[:, 0:K * P].rearrange("p (k c) -> p k c", k=K)).then_inc(flat, 1)

        @block.tensor
        def _(pe):
            pe.wait_ge(loaded, 16 * count[0])
            with pe.Fori(0, NG) as g:
                pe.wait_ge(slotted, g * K + K)
                for k in range(K):
                    last = nc.tensor.transpose(psT[:, k * P:(k + 1) * P], slot[:, k, :], m["ident"][:, :])
                last.then_inc(turned, 1)
                pe.wait_ge(flat, g + 1)
                pe.wait_ge(zeroed, g + K + 1)
                for k in range(K):
                    last = nc.tensor.matmul(psO[:, 0:4 * width], slotT[:, k, :], wb[k][:, :, :].rearrange("p b w -> p (b w)"),
                                            start=(k == 0), stop=(k == K - 1))
                last.then_inc(made, 1)

        @block.vector
        def _(dve):
            v = nc.vector
            n = Steps()
            link = linker(dve, dv, n)
            for k in range(K):
                v.memset(wb[k][:, :, :], 0.0).then_inc(zeroed, 1)
            dve.wait_ge(loaded, 16 * count[0])
            dve.sem_inc(zeroed, 1)
            with dve.Fori(0, NG) as g:
                n.enter(g, steps)
                dve.wait_ge(made, g + 1)
                finish(v, link, bass.ds(g * 4, 4), psO[:, 0:4 * width].rearrange("p (b w) -> p b w", b=4))
                dve.sem_inc(zeroed, 1)
            n.leave(NG)


def blocks_of(src):
    def weight(sp, k, wb, loaded):
        total = 0
        for piece, col in src[k]:
            for b in range(4):
                sp.dma_start(wb[D * b:D * b + D, b, col:col + piece.shape[1]], piece).then_inc(loaded, 16)
                total += 1
        return total
    return weight


def self_interaction(nc, m, a):
    def weight(sp, k, wb, loaded):
        for b in range(4):
            sp.dma_start(wb[D * b:D * b + MUL, b, 0:MUL], a["si0"]).then_inc(loaded, 16)
            for x in range(3):
                with nc.allow_non_contiguous_dma(reason="8 x 8 numbers"):
                    sp.dma_start(wb[D * b + MUL + x:D * b + D:3, b, MUL + x:D:3], a["si1"]).then_inc(loaded, 16)
        return 16

    def finish(v, link, at, ps):
        link(v.scalar_tensor_tensor(m["H"][:, at, :], ps, SI_SCALE, m["agg"][:, at, :], ALU.mult, ALU.add))
        link(v.tensor_tensor(m["X"][:, at, :], m["X"][:, at, :], m["H"][:, at, :], ALU.add))
    dense(nc, m, "si", [m["H"]], D, weight, finish, 2)


def mean_layer(nc, m, a):
    with Phase(nc, "ml") as ph:
        bias = ph.sb("bias", [P, 4, D])
        dv = ph.sem("dv")
        with nc.Block() as block:
            @block.vector
            def _(dve):
                nc.vector.tensor_tensor(m["agg"][:, :, :], m["agg"][:, :, :],
                                        m["cinv"][:, :, None].to_broadcast([P, NB, D]), ALU.mult).then_inc(dv, 1)

        def finish(v, link, at, ps):
            link(v.tensor_tensor(m["H"][:, at, :], ps, bias[:, :, :], ALU.add))
            link(v.scalar_tensor_tensor(m["X"][:, at, :], m["H"][:, at, :], 0.0, m["X"][:, at, :], ALU.max, ALU.add))
        extra = [(bias[:, b, :], a["bs"].to_broadcast([P, D])) for b in range(4)]
        dense(nc, m, "md", [m["H"], m["agg"]], D, blocks_of([[(a["Ws"][0:D, :], 0)], [(a["Ws"][D:2 * D, :], 0)]]), finish, 2, extra)


def attention_inputs(nc, m, a):
    with Phase(nc, "kv") as ph:
        kv = ph.sb("kv", [P, NB, 2 * D])

        def finish(v, link, at, ps):
            link(v.tensor_copy(m["agg"][:, at, :], ps[:, :, 0:D]))
            link(v.tensor_copy(kv[:, at, :], ps[:, :, D:3 * D]))
        dense(nc, m, "qd", [m["H"]], 3 * D, blocks_of([[(a["Wq"], 0), (a["Wk"], D), (a["Wv"], 2 * D)]]), finish, 2)
        store_rows(nc, "sq", m["QT"], m["agg"], D)
        store_rows(nc, "sk", m["KV"], kv, 2 * D)


def attention_pass(nc, m, a, *spread):
    W = D + 1
    with Phase(nc, "at") as ph:
        starts = Starts(m, ph, *spread)
        ix = ph.sb("ix", [P, 2, C], I32)
        g = ph.sb("g", [P, 2, C, 2 * D])
        ex = ph.sb("ex", [P, 2, C, D])
        same = ph.sb("same", [P, D, S1])
        qm = ph.sb("qm", [P, D, S1])
        qo = ph.sb("qo", [P, D, S1])
        prod = ph.sb("prod", [P, C, D])
        sc, neg, dl, sd, er, ew = (ph.sb(k, [P, C]) for k in ("sc", "neg", "dl", "sd", "er", "ew"))
        mx = ph.sb("mx", [P, S1])
        keep = ph.sb("keep", [P, W, S1])
        msg = ph.sb("msg", [P, W, S1])
        out = ph.sb("out", [P, W, S1])
        rows = ph.sb("rows", [P, C, W + 1])
        names = ("free", "begun", "spread", "queries", "scanned", "packed", "stored", "zs", "dv", "diffs", "exps")
        free, begun, spread, queries, scanned, packed, stored, zs, dv, diffs, exps = (ph.sem(k) for k in names)
        ixin = [ph.sem(f"ixin{b}") for b in range(2)]
        got = [ph.sem(f"got{b}") for b in range(2)]
        exin = [ph.sem(f"exin{b}") for b in range(2)]
        block = ph.ctx.enter_context(nc.Block())
        scv = m["SC34"][0:EP, :].rearrange("(p t) f -> p t f", p=P)
        exv = m["EX"][0:EP, :].rearrange("(p t) f -> p t f", p=P)
        srcv = m["src"].rearrange("(p t) -> p t", p=P)

        @block.sync
        def _(sp):
            for b in range(2):
                sp.wait_ge(free, b + 1)
                sp.dma_start(ix[:, b, :], srcv[:, b * C:(b + 1) * C]).then_inc(ixin[b], 16)
            sp.wait_ge(starts.put, 16 * NB)
            for b in range(2):
                sp.dma_start(ex[:, b, :, :], exv[:, b * C:(b + 1) * C, :]).then_inc(exin[b], 16)
            with sp.Fori(1, ROUNDS) as i:
                for b in range(2):
                    at = bass.ds((i * 2 + b) * C, C)
                    sp.wait_ge(free, i * 2 + b + 1)
                    sp.dma_start(ix[:, b, :], srcv[:, at]).then_inc(ixin[b], 16)
                    sp.dma_start(ex[:, b, :, :], exv[:, at, :]).then_inc(exin[b], 16)

        @block.gpsimd
        def _(pool):
            gather_rows(pool, ix, g, m["KV"], ixin, got, free, begun, starts=starts)

        @block.scalar
        def _(act):
            act.wait_ge(zs, 5)
            with act.Fori(0, ROUNDS) as i:
                for b in range(2):
                    nc.scalar.copy(same[:, :, 1:S1],
                                   m["same"][:, None, bass.ds((i * 2 + b) * C, C)].to_broadcast([P, D, C])).then_inc(spread, 1)
                    act.wait_ge(exin[b], i * 16 + 16)
                    nc.scalar.copy(qm[:, :, 1:S1], ex[:, b, :, :].rearrange("p c f -> p f c")).then_inc(queries, 1)
                    act.wait_ge(diffs, i * 4 + b * 2 + 2)
                    nc.scalar.activation(er[:, :], dl[:, :], ACT.Exp).then_inc(exps, 1)
                    nc.scalar.activation(ew[:, :], sd[:, :], ACT.Exp).then_inc(exps, 1)
                    act.wait_ge(scanned, i * 4 + b * 2 + 2)
                    nc.scalar.copy(rows[:, :, 0:W], out[:, :, 1:S1].rearrange("p f c -> p c f")).then_inc(packed, 1)
                    nc.scalar.copy(rows[:, :, W:W + 1], mx[:, 1:S1][:, :, None]).then_inc(packed, 1)
                    act.wait_ge(packed, i * 4 + b * 2 + 2)
                    act.dma_start(scv[:, bass.ds((i * 2 + b) * C, C), :], rows[:, :, :]).then_inc(stored, 16)
                    act.wait_ge(stored, i * 32 + (b + 1) * 16)

        @block.vector
        def _(dve):
            v = nc.vector
            n = Steps()
            link = linker(dve, dv, n)
            dve.sem_inc(free, 2)
            v.memset(same[:, :, 0:1], 0.0).then_inc(zs, 1)
            v.memset(keep[:, :, 0:1], 0.0).then_inc(zs, 1)
            v.memset(out[:, :, C:S1], 0.0).then_inc(zs, 1)
            v.memset(mx[:, C:S1], -BIG).then_inc(zs, 1)
            dve.wait_ge(starts.got, 16)
            v.tensor_copy(qo[:, :, C:S1], m["first"][:, :, None]).then_inc(zs, 1)
            dve.wait_ge(zs, 5)
            with dve.Fori(0, ROUNDS) as i:
                n.enter(i, 2 * 13)
                for b in range(2):
                    at = bass.ds((i * 2 + b) * C, C)
                    link(v.tensor_copy(qm[:, :, 0:1], qo[:, :, C:S1]))
                    dve.wait_ge(spread, i * 2 + b + 1)
                    dve.wait_ge(queries, i * 2 + b + 1)
                    v.tensor_tensor_scan(qo[:, :, :].rearrange("p f c -> p (f c)"), same[:, :, :].rearrange("p f c -> p (f c)"),
                                         qm[:, :, :].rearrange("p f c -> p (f c)"), 0.0, ALU.mult, ALU.add).then_inc(scanned, 1)
                    dve.wait_ge(scanned, i * 4 + b * 2 + 1)
                    dve.wait_ge(got[b], i * (16 * C) + 16 * C)
                    link(v.tensor_tensor(prod[:, :, :], qo[:, :, 1:S1].rearrange("p f c -> p c f"), g[:, b, :, 0:D], ALU.mult))
                    link(v.tensor_reduce(sc[:, :], prod[:, :, :], AX, ALU.add))
                    link(v.tensor_scalar(sc[:, :], sc[:, :], D ** -0.5, None, ALU.mult))
                    link(v.tensor_scalar(neg[:, :], m["same"][:, at], BIG, -BIG, ALU.mult, ALU.add))
                    link(v.tensor_copy(mx[:, 0:1], mx[:, C:S1]))
                    link(v.tensor_tensor_scan(mx[:, 1:S1], neg[:, :], sc[:, :], mx[:, 0:1], ALU.add, ALU.max))
                    link(v.tensor_tensor(dl[:, :], mx[:, 0:C], mx[:, 1:S1], ALU.subtract))
                    v.tensor_scalar(dl[:, :], dl[:, :], 0.0, None, ALU.min).then_inc(diffs, 1)
                    v.tensor_tensor(sd[:, :], sc[:, :], mx[:, 1:S1], ALU.subtract).then_inc(diffs, 1)
                    dve.wait_ge(exps, i * 4 + b * 2 + 2)
                    link(v.tensor_tensor(er[:, :], er[:, :], m["same"][:, at], ALU.mult))
                    link(v.tensor_copy(keep[:, :, 1:S1], er[:, None, :].to_broadcast([P, W, C])))
                    link(v.tensor_copy(msg[:, D:W, 1:S1], ew[:, None, :]))
                    link(v.tensor_tensor(msg[:, 0:D, 1:S1].rearrange("p f c -> p c f"), g[:, b, :, D:2 * D],
                                         ew[:, :, None].to_broadcast([P, C, D]), ALU.mult))
                    dve.sem_inc(free, 1)
                    link(v.tensor_copy(msg[:, :, 0:1], out[:, :, C:S1]))
                    v.tensor_tensor_scan(out[:, :, :].rearrange("p f c -> p (f c)"), keep[:, :, :].rearrange("p f c -> p (f c)"),
                                         msg[:, :, :].rearrange("p f c -> p (f c)"), 0.0, ALU.mult, ALU.add).then_inc(scanned, 1)
                    dve.wait_ge(scanned, i * 4 + b * 2 + 2)
                    dve.wait_ge(packed, i * 4 + b * 2 + 2)
            n.leave(ROUNDS)
            link(v.tensor_copy(m["last"][:, 0:W], out[:, :, C]))
            link(v.tensor_copy(m["last"][:, W:W + 1], mx[:, C:S1]))


def attention_collect(nc, m):
    W = D + 1
    with Phase(nc, "ac") as ph:
        pad = ph.sb("pad", [P, 3, P])
        padT = ph.sb("padT", [P, 3, P])
        neg, fa, fr = (ph.sb(k, [P, P]) for k in ("neg", "fa", "fr"))
        cm, ca = ph.sb("cm", [P, P + 1]), ph.sb("ca", [P, P + 1])
        row, car, merged = (ph.sb(k, [P, W + 1]) for k in ("row", "car", "merged"))
        wts = ph.sb("wts", [P, 2])
        rows = ph.sb("rows", [P, NB, W + 1])
        den = ph.sb("den", [P, NB])
        psT = ph.ps("psT", [P, 512])
        psC = ph.ps("psC", [P, 512])
        names = ("dv", "ready", "turned", "facin", "facs", "scanned", "back", "read", "merge", "put", "diffs", "exps", "got")
        dv, ready, turned, facin, facs, scanned, back, read, merge, put, diffs, exps, got = (ph.sem(k) for k in names)
        block = ph.ctx.enter_context(nc.Block())

        @block.vector
        def _(dve):
            v = nc.vector
            link = linker(dve, dv, Steps())
            link(v.memset(pad[:, :, :], 0.0))
            link(v.memset(ca[:, :], 0.0))
            link(v.memset(cm[:, :], -BIG))
            v.tensor_copy(pad[:, 0, 0:W], m["last"][:, 0:W]).then_inc(ready, 1)
            v.tensor_copy(pad[:, 1, 0:W], m["last"][:, W:W + 1].to_broadcast([P, W])).then_inc(ready, 1)
            v.tensor_copy(pad[:, 2, 0:W], m["whole"][:, 0:1].to_broadcast([P, W])).then_inc(ready, 1)
            dve.wait_ge(turned, 3)
            link(v.tensor_copy(padT[:, :, :], psT[:, 0:3 * P].rearrange("p (k c) -> p k c", k=3)))
            link(v.tensor_scalar(neg[:, :], padT[:, 2, :], BIG, -BIG, ALU.mult, ALU.add))
            link(v.tensor_tensor_scan(cm[:, 1:P + 1], neg[:, :], padT[:, 1, :], -BIG, ALU.add, ALU.max))
            v.tensor_tensor(fa[:, :], padT[:, 1, :], cm[:, 1:P + 1], ALU.subtract).then_inc(facin, 1)
            link(v.tensor_tensor(fr[:, :], cm[:, 0:P], cm[:, 1:P + 1], ALU.subtract))
            v.tensor_scalar(fr[:, :], fr[:, :], 0.0, None, ALU.min).then_inc(facin, 1)
            dve.wait_ge(facs, 2)
            link(v.tensor_tensor(fa[:, :], fa[:, :], padT[:, 0, :], ALU.mult))
            link(v.tensor_tensor(fr[:, :], fr[:, :], padT[:, 2, :], ALU.mult))
            v.tensor_tensor_scan(ca[:, 1:P + 1], fr[:, :], fa[:, :], 0.0, ALU.mult, ALU.add).then_inc(scanned, 1)
            dve.wait_ge(back, 2)
            link(v.tensor_copy(car[:, 0:W], psC[:, 0:W]))
            link(v.tensor_copy(car[:, W:W + 1], psC[:, P:P + 1]))
            dve.wait_ge(read, 16)
            link(v.tensor_tensor(merged[:, W:W + 1], row[:, W:W + 1], car[:, W:W + 1], ALU.max))
            v.tensor_tensor(wts[:, 0:1], row[:, W:W + 1], merged[:, W:W + 1], ALU.subtract).then_inc(diffs, 1)
            v.tensor_tensor(wts[:, 1:2], car[:, W:W + 1], merged[:, W:W + 1], ALU.subtract).then_inc(diffs, 1)
            dve.wait_ge(exps, 1)
            link(v.tensor_scalar(row[:, 0:W], row[:, 0:W], wts[:, 0:1], None, ALU.mult))
            v.scalar_tensor_tensor(merged[:, 0:W], car[:, 0:W], wts[:, 1:2], row[:, 0:W], ALU.mult, ALU.add).then_inc(merge, 1)
            dve.wait_ge(got, 16 * NB)
            link(v.tensor_scalar(den[:, :], rows[:, :, D], 1e-6, None, ALU.add))
            link(v.reciprocal(den[:, :], den[:, :]))
            link(v.tensor_tensor(m["agg"][:, :, :], rows[:, :, 0:D], den[:, :, None].to_broadcast([P, NB, D]), ALU.mult))

        @block.scalar
        def _(act):
            act.wait_ge(facin, 2)
            nc.scalar.activation(fa[:, :], fa[:, :], ACT.Exp).then_inc(facs, 1)
            nc.scalar.activation(fr[:, :], fr[:, :], ACT.Exp).then_inc(facs, 1)
            act.wait_ge(diffs, 2)
            nc.scalar.activation(wts[:, :], wts[:, :], ACT.Exp).then_inc(exps, 1)

        @block.tensor
        def _(pe):
            pe.wait_ge(ready, 3)
            for k in range(3):
                nc.tensor.transpose(psT[:, k * P:(k + 1) * P], pad[:, k, :], m["ident"][:, :]).then_inc(turned, 1)
            pe.wait_ge(scanned, 1)
            nc.tensor.transpose(psC[:, 0:P], ca[:, 0:P], m["ident"][:, :]).then_inc(back, 1)
            nc.tensor.transpose(psC[:, P:2 * P], cm[:, 0:P], m["ident"][:, :]).then_inc(back, 1)

        @block.gpsimd
        def _(pool):
            to = bass.IndirectOffsetOnAxis(ap=m["ixPatch"][:, 0:1], axis=0)
            pool.indirect_dma_start(out=row[:, :], out_offset=None, in_=m["SC34"], in_offset=to).then_inc(read, 16)
            pool.wait_ge(merge, 1)
            pool.indirect_dma_start(out=m["SC34"], out_offset=to, in_=merged[:, :], in_offset=None).then_inc(put, 16)
            pool.wait_ge(put, 16)
            for j in range(NB):
                pool.indirect_dma_start(out=rows[:, j, :], out_offset=None, in_=m["SC34"],
                                        in_offset=bass.IndirectOffsetOnAxis(ap=m["ixEnd"][:, j:j + 1], axis=0)).then_inc(got, 16)
            pool.wait_ge(got, 16 * NB)


def attention_output(nc, m, a):
    def finish(v, link, at, ps):
        link(v.tensor_tensor(m["H"][:, at, :], m["H"][:, at, :], ps, ALU.add))
        link(v.tensor_tensor(m["X"][:, at, :], m["X"][:, at, :], m["H"][:, at, :], ALU.add))
    dense(nc, m, "ao", [m["agg"]], D, blocks_of([[(a["Wo"], 0)]]), finish, 2)


def load_x(nc, m, a):
    with Phase(nc, "lx") as ph:
        landed = ph.sem("landed")
        block = ph.ctx.enter_context(nc.Block())

        @block.sync
        def _(sp):
            sp.dma_start(m["X"][:, :, :], a["x"].rearrange("(p j) f -> p j f", p=P)).then_inc(landed, 16)
            sp.dma_start(m["dst"][0:1].rearrange("(a t) -> a t", a=1), a["dst"][0:1].rearrange("(a t) -> a t", a=1)).then_inc(landed, 16)
            sp.dma_start(m["dst"][1 + EP:1 + EP + T].rearrange("(a t) -> a t", a=1),
                         a["dst"][1 + EP:1 + EP + T].rearrange("(a t) -> a t", a=1)).then_inc(landed, 16)
            sp.wait_ge(landed, 48)


def build(nc, a, out, stop=99):
    with ExitStack() as ctx:
        m = {}

        def sb(name, shape, dt=F32):
            m[name] = ctx.enter_context(nc.sbuf_tensor(name, shape, dt))

        def dram(name, shape, dt=F32):
            m[name] = nc.dram_tensor(name, shape, dt, kind="Internal").ap()
        for name in ("cnt", "deg", "dinv", "cinv", "tsum"):
            sb(name, [P, NB])
        for name in ("ixStart", "ixEnd"):
            sb(name, [P, NB], I32)
        for name in ("iota", "ident", "below", "above"):
            sb(name, [P, P])
        sb("iotab", [P, P], BF16)
        sb("rowid", [P, 1])
        sb("dst0", [P, 1], I32)
        sb("ixPatch", [P, 1], I32)
        sb("flag", [1, 1], I32)
        sb("whole", [P, 1])
        sb("last", [P, D + 2])
        sb("first", [P, D])
        sb("firstd", [P, 1])
        for name in ("X", "H", "agg"):
            sb(name, [P, NB, D])
        sb("same", [P, T])
        for name, width in (("HT", D), ("UT", D), ("QT", D), ("KV", 2 * D), ("DEG", 1)):
            dram(name, (NP, width))
        dram("SC", (EP + 1 + P, D))
        dram("SC34", (EP + 1 + P, D + 2))
        dram("EX", (EP + P, D))
        dram("EXD", (EP + P, 1))
        dram("src", (EP,), I32)
        dram("dst", (1 + EP + T,), I32)
        dram("sh", (EP, 4))
        dram("efT", (P, T // 4 * P))
        dram("BASE", (NP + P, 1))
        dram("REC", (EP, D + 6))
        for k in range(CHAINS):
            dram(f"ACC{k}", (ACCROWS, D))
        body(nc, m, a, out)


def body(nc, m, a, out):
    with nc.sbuf_tensor("srcf", [P, T], F32) as m["srcf"], nc.sbuf_tensor("zero", [P, ZW], F32) as m["zero"]:
        with nc.sbuf_tensor("dstf", [P, T], F32) as m["dstf"]:
            load_x(nc, m, a)
            constants(nc, m)
            check_order(nc, m, a)
            unordered = nc.values_load(m["flag"][0:1, 0:1], min_val=0, max_val=1)
            with nc.If(unordered != 0):
                nc.all_engine_barrier()
                load_edges(nc, m, "l0", a["src"], a["dst"])
                histogram(nc, m, "hd", m["dstf"], m["cnt"])
                node_indices(nc, m, "nd")
                place_edges(nc, m, a)
                unpack_edges(nc, m, a)
            with nc.Else():
                nc.all_engine_barrier()
                copy_ids(nc, m, a)
            load_edges(nc, m, "l1", m["src"], m["dst"])
            histogram(nc, m, "hs", m["srcf"], m["deg"], zero_scratch(m), copy_attributes(m, a, unordered == 0))
            degrees(nc, m)
            store_rows(nc, "dg", m["DEG"], m["deg"][:, :, None], 1)
            norm_relu(nc, m, "n0", m["X"], m["H"], m["HT"], m["dinv"])
            gather_pass(nc, m, "g0", m["HT"], m["src"], 0, JROUNDS, (m["dstf"], None, m["cnt"]))
        node_indices(nc, m, "ni")
        gather_pass(nc, m, "g1", m["HT"], m["src"], 2 * JROUNDS, ROUNDS - 2 * JROUNDS,
                    starts=(m["EXD"], lambda j: m["deg"][:, j:j + 1], m["DEG"], m["firstd"]))
        with nc.sbuf_tensor("wts", [P, T], F32) as m["wts"]:
            expand_degrees(nc, m)
            gather_pass(nc, m, "g2", m["HT"], m["src"], 2 * (ROUNDS - JROUNDS), JROUNDS, (m["srcf"], m["wts"], m["tsum"]))
        carry_and_collect(nc, m, "c0")
        hamilton_gradient(nc, m, a)
        store_rows(nc, "su", m["UT"], m["H"], D)
        scatter_to_starts(nc, m, "sx", m["EX"], lambda j: m["H"][:, j, :], m["UT"], m["first"])
        scatter_pass(nc, m)
        add_gradient(nc, m)
    norm_relu(nc, m, "n1", m["X"], m["H"], m["HT"])
    product_pass(nc, m, a)
    carry_and_collect(nc, m, "c1")
    self_interaction(nc, m, a)
    norm_relu(nc, m, "n2", m["X"], m["H"], m["HT"])
    gather_pass(nc, m, "g3", m["HT"], m["src"])
    carry_and_collect(nc, m, "c2")
    mean_layer(nc, m, a)
    norm_relu(nc, m, "n3", m["X"], m["H"], None)
    attention_inputs(nc, m, a)
    attention_pass(nc, m, a, m["EX"], lambda j: m["agg"][:, j, :], m["QT"], m["first"])
    attention_collect(nc, m)
    attention_output(nc, m, a)
    store_rows(nc, "st", out, m["X"], D)


def kernel(**inputs):
    import numpy as np
    import concourse.bacc as bacc
    from concourse.bass_utils import run_bass_kernel_spmd

    f = {k: np.asarray(v) for k, v in inputs.items()}
    arrays = {
        "x": np.concatenate([f["x"], np.zeros((NP - N, D), np.float32)]),
        "src": np.concatenate([f["src"], np.full(EP - E, NP - 1, np.int32)]),
        "dst": np.concatenate([np.full(1, -1, np.int32), f["dst"], np.full(EP - E, NP - 1, np.int32),
                               np.full(T, NP, np.int32)]),
    }
    sh = np.concatenate([f["edge_attr_4"], np.zeros((EP - E, 4), np.float32)])
    arrays["sh"] = np.ascontiguousarray(sh)
    ef = np.concatenate([f["edge_attr_32"], np.zeros((EP - E, D), np.float32)])
    arrays["efT"] = np.ascontiguousarray(ef.reshape(P, T // 4, 4, D).transpose(2, 3, 1, 0).reshape(P, T // 4 * P))
    arrays["erow"] = np.concatenate([sh, ef], axis=1)
    arrays["W1"] = f["L0_gnn_W1"]
    arrays["b1"] = f["L0_gnn_b1"].reshape(P, 1)
    arrays["W2"] = f["L0_gnn_W2"]
    arrays["JT"] = np.ascontiguousarray(f["L0_gnn_J"].T)
    arrays["V1"] = f["L1_gnn_W1"]
    arrays["c1"] = f["L1_gnn_b1"].reshape(HID1, 1)
    w2 = np.concatenate([f["L1_gnn_W2"], f["L1_gnn_b2"].reshape(1, WN)]).reshape(HID1 + 1, 4, MUL, MUL)
    w2 = w2.transpose(0, 1, 3, 2)
    pair = np.stack([w2[:, 0], w2[:, 3]], axis=2).reshape(HID1 + 1, 128)
    arrays["V2"] = np.concatenate([pair, w2[:, 1].reshape(HID1 + 1, 64), w2[:, 2].reshape(HID1 + 1, 64)], axis=1)
    arrays["si0"] = f["L1_gnn_si_w0"]
    arrays["si1"] = f["L1_gnn_si_w1"]
    arrays["Ws"] = f["L2_gnn_W"]
    arrays["bs"] = f["L2_gnn_b"].reshape(1, D)
    arrays["Wq"], arrays["Wk"] = f["L3_gnn_Wq"], f["L3_gnn_Wk"]
    arrays["Wv"], arrays["Wo"] = f["L3_gnn_Wv"], f["L3_gnn_Wo"]

    nc = bacc.Bacc("TRN2", target_bir_lowering=False, num_devices=1)
    arrays = {k: np.ascontiguousarray(v) for k, v in arrays.items()}
    a = {k: nc.dram_tensor(f"in_{k}", v.shape, mybir.dt.from_np(v.dtype), kind="ExternalInput").ap()
         for k, v in arrays.items()}
    out = nc.dram_tensor("out", (NP, D), F32, kind="ExternalOutput").ap()
    build(nc, a, out)
    r = run_bass_kernel_spmd(nc, [{f"in_{k}": v for k, v in arrays.items()}], core_ids=[0])
    return r.results[0]["out"][0:N]
```
